# Optimizing a Trainium2 kernel written in Bass

```python
import numpy as np
import jax
import jax.numpy as jnp

def _softmax(x, axis=-1):
    return jax.nn.softmax(x, axis=axis)
def _gelu(x):
    return jax.nn.gelu(x, approximate=True)
def _silu(x):
    return jax.nn.silu(x)
def _sigmoid(x):
    return jax.nn.sigmoid(x)
def _layernorm(x, axis=-1, eps=1e-5):
    m = jnp.mean(x, axis=axis, keepdims=True)
    v = jnp.var(x, axis=axis, keepdims=True)
    return (x - m) / jnp.sqrt(v + eps)
def _scatter_add(tgt, idx, src, axis=0):
    return tgt.at[idx].add(src)
def _segment_sum(src, seg, n):
    return jax.ops.segment_sum(src, seg, n)

kernel_name = 'mk_conv_seq_d1_conv_nchw256_a8ae09'

def setup_inputs(seed: int = 0):
    np.random.seed(seed)
    _w = jnp.asarray
    def _rec_inputs():
        import jax
        import jax.numpy as jnp
        _gk = jax.random.key(seed)
        x = -0.000125 + 0.9999 * jax.random.normal(jax.random.fold_in(_gk, 1), (8, 256, 128, 128), jnp.float32)
        return x
    x = _rec_inputs()
    def _L0_conv_setup():
        import jax, jax.numpy as jnp
        import numpy as np
        M = 7
        EPS = 1e-08

        def _aniso_kernels(params):
            theta = jnp.arctan2(params[:, 0], params[:, 1]) / 2.0 + jnp.pi / 2.0
            lam1 = jnp.exp(params[:, 2])
            lam2 = 1.0 / (lam1 + EPS)
            lin = jnp.linspace(-(M // 2), M // 2, M, dtype=params.dtype)
            yy, xx = jnp.meshgrid(lin, lin, indexing='ij')
            cos_t = jnp.cos(theta)[:, None, None]
            sin_t = jnp.sin(theta)[:, None, None]
            x_rot = xx * cos_t + yy * sin_t
            y_rot = -xx * sin_t + yy * cos_t
            k = jnp.exp(-(x_rot ** 2 / (2.0 * lam1[:, None, None] ** 2) + y_rot ** 2 / (2.0 * lam2[:, None, None] ** 2)))
            return k / (k.sum(axis=(1, 2), keepdims=True) + EPS)
        key = jax.random.key(seed)
        ks = jax.random.split(key, 6)
        B, C, H, W = (8, 256, 128, 128)
        return {'x': jax.random.normal(ks[0], (B, C, H, W), dtype=jnp.float32), 'w1': jax.random.normal(ks[1], (M * M, 32), dtype=jnp.float32) * 0.1, 'b1': jnp.zeros((32,), dtype=jnp.float32), 'w2': jax.random.normal(ks[2], (32, 3), dtype=jnp.float32) * 0.1, 'b2': jnp.zeros((3,), dtype=jnp.float32), 'wr': jax.random.normal(ks[3], (256, 256), dtype=jnp.float32) * (1.0 / 16.0)}
    _L0_conv_all = _L0_conv_setup()
    _L0_conv_in = {k: v for k, v in _L0_conv_all.items() if k in ('w1', 'b1', 'w2', 'b2', 'wr', )}
    del _L0_conv_all

    return {
        "x": x,
        "L0_conv_w1": _L0_conv_in["w1"],
        "L0_conv_b1": _L0_conv_in["b1"],
        "L0_conv_w2": _L0_conv_in["w2"],
        "L0_conv_b2": _L0_conv_in["b2"],
        "L0_conv_wr": _L0_conv_in["wr"],
    }

def reference(x, L0_conv_w1, L0_conv_b1, L0_conv_w2, L0_conv_b2, L0_conv_wr):
    import jax
    import jax.numpy as jnp
    def _L0_conv_ref(x, w1, b1, w2, b2, wr):
        import jax, jax.numpy as jnp
        import numpy as np
        M = 7
        EPS = 1e-08

        def _aniso_kernels(params):
            theta = jnp.arctan2(params[:, 0], params[:, 1]) / 2.0 + jnp.pi / 2.0
            lam1 = jnp.exp(params[:, 2])
            lam2 = 1.0 / (lam1 + EPS)
            lin = jnp.linspace(-(M // 2), M // 2, M, dtype=params.dtype)
            yy, xx = jnp.meshgrid(lin, lin, indexing='ij')
            cos_t = jnp.cos(theta)[:, None, None]
            sin_t = jnp.sin(theta)[:, None, None]
            x_rot = xx * cos_t + yy * sin_t
            y_rot = -xx * sin_t + yy * cos_t
            k = jnp.exp(-(x_rot ** 2 / (2.0 * lam1[:, None, None] ** 2) + y_rot ** 2 / (2.0 * lam2[:, None, None] ** 2)))
            return k / (k.sum(axis=(1, 2), keepdims=True) + EPS)
        B, C, H, W = x.shape
        xf = jnp.fft.fftshift(jnp.fft.fft2(x, norm='ortho'), axes=(-2, -1))
        mag = jnp.abs(xf).mean(axis=1)
        h0, w0 = (H // 2 - M // 2, W // 2 - M // 2)
        center = mag[:, h0:h0 + M, w0:w0 + M].reshape(B, M * M)
        hid = jax.nn.relu(center @ w1 + b1)
        params = hid @ w2 + b2
        kern = _aniso_kernels(params)
        stacked = jnp.concatenate([xf.real, xf.imag], axis=1)
        pad = [(M // 2, M // 2)] * 2

        def conv_one(img, k):
            return jax.lax.conv_general_dilated(img[:, None], k[None, None], (1, 1), pad)[:, 0]
        filt = jax.vmap(conv_one)(stacked, kern)
        real_f, imag_f = (filt[:, :C], filt[:, C:])
        rr = jnp.einsum('bchw,oc->bohw', real_f, wr)
        ii = jnp.einsum('bchw,oc->bohw', imag_f, wr)
        out_f = jnp.fft.ifftshift(jax.lax.complex(rr, ii), axes=(-2, -1))
        return jnp.fft.ifft2(out_f, norm='ortho').real + x

    def _gn(v, G=32, eps=1e-5):
        B_, C_, H_, W_ = v.shape
        g = v.reshape(B_, G, C_ // G, H_, W_)
        m = jnp.mean(g, axis=(2, 3, 4), keepdims=True)
        s = jnp.var(g, axis=(2, 3, 4), keepdims=True)
        return ((g - m) / jnp.sqrt(s + eps)).reshape(v.shape)

    def _ln_c(v, eps=1e-6):
        m = jnp.mean(v, axis=1, keepdims=True)
        s = jnp.var(v, axis=1, keepdims=True)
        return (v - m) / jnp.sqrt(s + eps)

    def _ln_t(v, eps=1e-5):
        m = jnp.mean(v, axis=-1, keepdims=True)
        s = jnp.var(v, axis=-1, keepdims=True)
        return (v - m) / jnp.sqrt(s + eps)

    def _to_tokens(v):
        B_, C_, H_, W_ = v.shape
        return v.reshape(B_, C_, H_ * W_).transpose(0, 2, 1)
    def _from_tokens(t, like):
        B_, C_, H_, W_ = like.shape
        return t.transpose(0, 2, 1).reshape(B_, C_, H_, W_)

    x = _L0_conv_ref(x, L0_conv_w1, L0_conv_b1, L0_conv_w2, L0_conv_b2, L0_conv_wr)
    return x


_drawn_inputs = setup_inputs


def setup_inputs(seed=0):
    import zlib

    import numpy as np

    out = dict(_drawn_inputs(seed))
    spreads = {'L0_conv_b1': (0.0, 0.324), 'L0_conv_b2': (0.0, 0.1)}
    factors = {'L0_conv_w1': 4.141}
    for name, (base, spread) in spreads.items():
        noise = np.random.default_rng([zlib.crc32(name.encode()), seed]).standard_normal(out[name].shape)
        drawn = base * np.exp(spread * noise) if base else spread * noise
        out[name] = jnp.asarray(drawn.astype(out[name].dtype))
    for name, factor in factors.items():
        out[name] = (out[name] * factor).astype(out[name].dtype)
    return out
```

```python
from contextlib import ExitStack

import numpy as np

import concourse.bass as bass
from concourse import mybir

F32 = mybir.dt.float32
BF16 = mybir.dt.bfloat16
ALU = mybir.AluOpType
ACT = mybir.ActivationFunctionType
AX = mybir.AxisListType

P = 128
NB, C, H, W = 8, 256, 128, 128
KS = 7
R = 3
EPS = 1e-8
TH = 2.0 * np.pi / 128
CH = C // P
NR = 7
GROUPS = 16
TILES = 32
ROWS = H // TILES
XS = 4
OS = 3
QC = 16
CHUNKS = C // QC
REPS = 6
KROWS = REPS * 2 * NR
PARTS = [(0, 0), (0, 1), (0, 2), (1, 0), (1, 1), (2, 0)]
CENTRE_PAIRS = 25
TERMS = [(0, 1, 0, 1, 1), (0, -1, 1, 1, 2), (0, 1, 0, 2, 3), (0, -1, 1, 2, 4), (0, 1, 0, 3, 5), (0, -1, 1, 3, 6),
         (1, 1, 0, 1, 0), (1, 2, 0, 2, 1), (1, -2, 1, 2, 2), (1, 2, 0, 3, 3), (1, -2, 1, 3, 4),
         (2, -1, 1, 1, 0), (2, -2, 0, 2, 2), (2, -2, 1, 2, 1), (2, -2, 0, 3, 4), (2, -2, 1, 3, 3),
         (3, 1, 0, 2, 0), (3, 2, 0, 3, 1), (3, -2, 1, 3, 2),
         (4, -1, 1, 2, 0), (4, -2, 0, 3, 2), (4, -2, 1, 3, 1),
         (5, 1, 0, 3, 0), (6, -1, 1, 3, 0)]
SCALES = [-1, 1, -2, 2]


def term_rounds():
    rounds, left = [], list(TERMS)
    while left:
        seen, now = set(), []
        for t in list(left):
            if t[0] not in seen:
                seen.add(t[0])
                now.append(t)
                left.remove(t)
        rounds.append(now)
    return rounds


ROUNDS = term_rounds()


def waves(sign):
    n = np.arange(P)
    s = np.where(n % 2 == 1, float(sign), 1.0)
    cols = [s]
    for q in range(1, R + 1):
        cols += [s * np.cos(TH * q * n), s * np.sin(TH * q * n)]
    return np.stack(cols, 1)


def wrapped():
    v = np.zeros((KS, NR, NR), complex)

    def wave(q, s):
        u = np.zeros(NR, complex)
        if q == 0:
            u[0] = 1
        else:
            u[2 * abs(q) - 1] = 1
            u[2 * abs(q)] = s * 1j * np.sign(q)
        return u

    for j in range(-R, R + 1):
        for q in range(-R, R + 1):
            src = q + j
            if -R <= src <= R and ((j > 0 and q < 0 <= src) or (j < 0 and q >= 0 > src)):
                v[j + R] += np.outer(wave(q, 1), wave(src, -1)) / P
    return v


CORNER_PAIRS = [(a, b) for a in range(R + 1, KS) for b in range(KS) if b != R]


def bf16_bits(a):
    bits = a.astype(np.float32).view(np.uint32).astype(np.uint64)
    return ((bits + 0x7FFF + ((bits >> 16) & 1)) >> 16).astype(np.uint16)


def bf16_parts(a):
    parts, rest = [], a.astype(np.float64)
    for _ in range(3):
        p = (bf16_bits(rest).astype(np.uint32) << 16).view(np.float32).astype(np.float64)
        parts.append(p)
        rest = rest - p
    return parts


def tables():
    low, nyq = waves(1), waves(-1)
    m, d = np.arange(P), np.arange(-R, R + 1)
    proj_n = np.zeros((P, 32))
    proj_n[:, 0:NR], proj_n[:, NR:2 * NR] = low, nyq
    proj_m = np.zeros((P, 32))
    proj_m[:, 0:NR] = nyq
    trig = np.stack([np.cos(TH * np.outer(d, m)), np.sin(TH * np.outer(d, m))], 1)
    xx, yy = np.zeros((P, 63)), np.zeros((P, 63))
    f = np.arange(49)
    xx[:, :49], yy[:, :49] = f % KS - R, f // KS - R
    xx[:KS, 49:56], yy[:KS, 49:56] = d[None, :], d[:, None]
    xx[:KS, 56:63], yy[:KS, 56:63] = d[:, None], d[None, :]
    v = wrapped()
    corner = np.zeros((49, len(CORNER_PAIRS), 49))
    for i, (a, b) in enumerate(CORNER_PAIRS):
        for aa, bb in ((a, b), (KS - 1 - a, KS - 1 - b)):
            t = np.einsum("rp,sq->pqrs", v[aa], v[bb]).real
            corner[:, i, :] += t.reshape(49, 49)
    e = [p.T for p in bf16_parts(nyq)]
    waves_n = np.zeros((REPS, 2, NR, P))
    waves_m = np.zeros((REPS, 2, NR, P))
    for i, (_, part) in enumerate(PARTS):
        waves_n[i, 0] = e[part]
        waves_m[i, 1] = e[part]
    waves_n, waves_m = waves_n.reshape(KROWS, P), waves_m.reshape(KROWS, P)
    f32 = lambda a: np.ascontiguousarray(a.astype(np.float32))
    bf = lambda a: np.ascontiguousarray(bf16_bits(a))
    return {
        "proj_n": f32(proj_n), "proj_m": f32(proj_m), "nyq_t": f32(nyq.T), "trig": f32(trig),
        "grid": f32(np.stack([xx, yy], 1)), "corner": f32(corner), "ident": f32(np.eye(P)),
        "ident_bf": bf(np.eye(P)), "waves_n": bf(waves_n), "waves_m": bf(waves_m),
    }


def build(nc, x, w1a, w1b, b1, w2, b2, wrt, tab, out):
    with ExitStack() as ctx:
        def sb(name, shape, dt=F32):
            return ctx.enter_context(nc.sbuf_tensor(name, shape, dt))

        def sem(name):
            return ctx.enter_context(nc.semaphore(name))

        zt = sb("zt", [P, H, C])
        xin = sb("xin", [P, XS, 1024])
        shared = sb("shared", [P, OS * 1024])
        xo = shared[:, :].rearrange("p (s f) -> p s f", s=OS)
        parts = [shared[:, i * 672:(i + 1) * 672].bitcast(BF16).rearrange("p (o k r) -> p o k r", o=QC, k=REPS)
                 for i in range(2)]
        spread = shared[0:KROWS, 1344:2368].bitcast(BF16).rearrange("p (o f) -> p o f", o=QC)
        rest = shared[:, 2368:2816].rearrange("p (s o r) -> p s o r", s=2, o=QC)
        beta = sb("beta", [P, 2 * NR, C])
        gd = sb("gd", [P, 2 * NR, C])
        dproj = sb("dproj", [P, NR, C])
        raw = sb("raw", [P, 2, 512])
        proj_n = sb("proj_n_sb", [P, 32])
        proj_m = sb("proj_m_sb", [P, 32])
        nyq_t = sb("nyq_t_sb", [NR, P])
        trig = sb("trig_sb", [KS, 2, P])
        grid = sb("grid_sb", [P, 2, 63])
        corner = sb("corner_sb", [49, len(CORNER_PAIRS), 49])
        ident = sb("ident_sb", [P, P])
        ident_bf = sb("ident_bf_sb", [P, P], BF16)
        waves_n = sb("waves_n_sb", [KROWS, P], BF16)
        waves_m = sb("waves_m_sb", [KROWS, P], BF16)
        wrt_sb = sb("wrt_sb", [P, CH, C])
        w1a_sb = sb("w1a_sb", [CENTRE_PAIRS, 32])
        w1b_sb = sb("w1b_sb", [CENTRE_PAIRS - 1, 32])
        b1_sb = sb("b1_sb", [32, 1])
        w2_sb = sb("w2_sb", [32, 3])
        b2_sb = sb("b2_sb", [1, 3])
        ones = sb("ones", [32, P])
        mean = sb("mean", [P, 1])
        pc = sb("pc", [P, 40])
        kn = sb("kn", [P, 2, len(SCALES), 6])
        wt = sb("wt", [P, H])
        cen = sb("cen", [CENTRE_PAIRS, 1])
        hid = sb("hid", [32, 1])
        flat = dproj[:, :, :].rearrange("p r o -> p (r o)")
        taken = [0]

        def scratch(rows, n):
            taken[0] += n
            assert taken[0] <= NR * C
            return flat[0:rows, taken[0] - n:taken[0]]

        spec = scratch(P, CH * 49).rearrange("p (h f) -> p h f", h=CH)
        re = scratch(P, CH * CENTRE_PAIRS).rearrange("p (h f) -> p h f", h=CH)
        im = scratch(P, CH * CENTRE_PAIRS).rearrange("p (h f) -> p h f", h=CH)
        mag = scratch(P, CH * CENTRE_PAIRS).rearrange("p (h f) -> p h f", h=CH)
        hid_rep = scratch(32, P)
        g1, g2, g3, g4 = (scratch(P, 63) for _ in range(4))
        kern = scratch(P, 63)
        ptab = scratch(KS, 2 * P).rearrange("p (t m) -> p t m", t=2)
        cmap = scratch(49, 49)
        eps_sb = scratch(P, CH * 49).rearrange("p (h f) -> p h f", h=CH)
        eps_t = scratch(49, C)

        ps = ctx.enter_context(nc.psum_tensor("ps", [P, 8, 512], F32))
        turned_parts = [ps[0:KROWS, 4 + i, :].bitcast(BF16).rearrange("p (o f) -> p o f", o=QC // 2) for i in range(2)]

        const_in = sem("const_in")
        const_set = sem("const_set")
        xin_in = [sem(f"xin_in{i}") for i in range(XS)]
        xres_in = [sem(f"xres_in{i}") for i in range(OS)]
        stored = [sem(f"stored{i}") for i in range(OS)]
        raw_mm, raw_sb, trn_mm, trn_sb = sem("raw_mm"), sem("raw_sb"), sem("trn_mm"), sem("trn_sb")
        z_mm, z_sb = sem("z_mm"), sem("z_sb")
        turn_mm, out_add = sem("turn_mm"), sem("out_add")
        wz_done = sem("wz_done")
        delta_done = sem("delta_done")
        gamma_done = sem("gamma_done")
        lead_set, rest_set, mid_set, low_set = sem("lead_set"), sem("rest_set"), sem("mid_set"), sem("low_set")
        split_mm, split_sb = sem("split_mm"), sem("split_sb")
        corr_mm, corr_add = sem("corr_mm"), sem("corr_add")
        bturn_mm, bturn_sb, bmix_mm, bmix_sb = sem("bturn_mm"), sem("bturn_sb"), sem("bmix_mm"), sem("bmix_sb")
        stat_mm, stat_sq, mag_set = sem("stat_mm"), sem("stat_sq"), sem("mag_set")
        cen_mm, cen_set, hid_mm, hid_set, par_mm = sem("cen_mm"), sem("cen_set"), sem("hid_mm"), sem("hid_set"), sem("par_mm")
        rsq_set, rad_set, hsq_set, half_set, lam_set = (sem("rsq_set"), sem("rad_set"), sem("hsq_set"),
                                                        sem("half_set"), sem("lam_set"))
        expo_set, exp_set, kern_set = sem("expo_set"), sem("exp_set"), sem("kern_set")
        tab_mm, tab_set, w_mm, w_set = sem("tab_mm"), sem("tab_set"), sem("w_mm"), sem("w_set")
        eps_mm, eps_set, epst_mm, epst_set, cmap_set = (sem("eps_mm"), sem("eps_set"), sem("epst_mm"),
                                                        sem("epst_set"), sem("cmap_set"))
        kap_mm, kap_sb, init_mm, init_sb = sem("kap_mm"), sem("kap_sb"), sem("init_mm"), sem("init_sb")
        dve_step = sem("dve_step")

        shared_free = sem("shared_free")
        turn_read = sem("turn_read")
        dproj_free = sem("dproj_free")
        passed = sem("passed")

        consts = [(proj_n, tab["proj_n"]), (proj_m, tab["proj_m"]), (nyq_t, tab["nyq_t"]), (trig, tab["trig"]),
                  (grid, tab["grid"]), (corner, tab["corner"]), (ident, tab["ident"]),
                  (ident_bf, tab["ident_bf"].bitcast(BF16)), (waves_n, tab["waves_n"].bitcast(BF16)),
                  (waves_m, tab["waves_m"].bitcast(BF16)), (wrt_sb, wrt),
                  (w1a_sb, w1a), (w1b_sb, w1b), (b1_sb, b1), (w2_sb, w2), (b2_sb, b2)]
        CONST_READY = 16 * len(consts)

        TURNS = 2 * TILES
        slot_tiles = [len(range(s, TILES, OS)) for s in range(OS)]
        ring_tiles = 2 * TILES // XS

        def front_base(k):
            return k * (2 * GROUPS)

        block_ctx = ctx.enter_context(nc.Block())

        def own_wait(engine):
            engine.sem_inc(passed, 1)

        @block_ctx.sync
        def _(sp):
            for dst, src in consts:
                sp.dma_start(dst[:], src).then_inc(const_in, 16)

            def front_load(k, first):
                for u in range(TILES):
                    if u >= XS:
                        sp.wait_ge(raw_mm, front_base(k) + (u - XS) // 2 + 1)
                    elif not first:
                        sp.wait_ge(z_mm, k * TURNS - 2 * (XS - u) + 2)
                    sp.dma_start(xin[:, u % XS, :].rearrange("p (c m) -> p c m", c=8),
                                 x[k, 8 * u:8 * u + 8, :, :].rearrange("c n m -> n c m")).then_inc(xin_in[u % XS], 16)

            def mix_load(k):
                for t in range(TILES):
                    if t >= XS:
                        sp.wait_ge(z_mm, k * TURNS + 2 * (t - XS) + 2)
                    else:
                        sp.wait_ge(raw_mm, front_base(k) + (TILES + t - XS) // 2 + 1)
                    sp.dma_start(xin[:, t % XS, :].rearrange("p (h f) -> p h f", h=CH),
                                 x[k, :, ROWS * t:ROWS * (t + 1), :].rearrange("(h c) n m -> c h (n m)", h=CH))\
                      .then_inc(xin_in[t % XS], 16)

            front_load(0, True)
            mix_load(0)
            with sp.Fori(0, NB - 1) as k:
                front_load(k + 1, False)
                mix_load(k + 1)

        @block_ctx.gpsimd
        def _(pool):
            def store(k, t):
                pool.wait_ge(out_add, k * TURNS + 2 * t + 2)
                own_wait(pool)
                pool.dma_start(out[k, :, ROWS * t:ROWS * (t + 1), :].rearrange("(h c) n m -> c h (n m)", h=CH),
                               xo[:, t % OS, :].rearrange("p (h f) -> p h f", h=CH)).then_inc(stored[t % OS], 16)

            def turn_io(k):
                pool.wait_ge(corr_mm, (k + 1) * 2 * CHUNKS)
                for t in range(TILES):
                    if t >= OS:
                        pool.wait_ge(stored[t % OS], 16 * (k * slot_tiles[t % OS] + t // OS))
                    own_wait(pool)
                    pool.dma_start(xo[:, t % OS, :].rearrange("p (h f) -> p h f", h=CH),
                                   x[k, :, ROWS * t:ROWS * (t + 1), :].rearrange("(h c) n m -> c h (n m)", h=CH))\
                        .then_inc(xres_in[t % OS], 16)
                    if t >= 1:
                        store(k, t - 1)
                store(k, TILES - 1)
                for s in range(OS):
                    pool.wait_ge(stored[s], 16 * (k + 1) * slot_tiles[s])
                pool.sem_inc(shared_free, 1)

            pool.sem_inc(shared_free, 1)
            with pool.Fori(0, NB - 1) as k:
                turn_io(k)
            turn_io(NB - 1)
            for s in range(OS):
                pool.wait_ge(stored[s], 16 * NB * slot_tiles[s])

        @block_ctx.tensor
        def _(pe):
            mm = nc.tensor.matmul
            tr = nc.tensor.transpose

            def turn_groups(base, stationary):
                def one(g):
                    pe.wait_ge(raw_sb, base + g + 1)
                    if g >= 2:
                        pe.wait_ge(trn_sb, base + g - 1)
                    for i in range(4):
                        last = tr(ps[:, 6 + g % 2, P * i:P * (i + 1)], stationary(g, i), ident[:])
                    last.then_inc(trn_mm, 1)
                return one

            def front(k):
                base = front_base(k)
                turn = turn_groups(base, lambda g, i: raw[:, g % 2, P * i:P * (i + 1)])
                for g in range(GROUPS):
                    if g >= 2:
                        pe.wait_ge(raw_sb, base + g - 1)
                    for j in range(4):
                        u = 2 * g + j // 2
                        if j % 2 == 0:
                            pe.wait_ge(xin_in[u % XS], 16 * (k * ring_tiles + u // XS + 1))
                        last = mm(ps[32 * j:32 * j + 32, 4 + g % 2, :], proj_n[:],
                                  xin[:, u % XS, 512 * (j % 2):512 * (j % 2) + 512], start=True, stop=True)
                    last.then_inc(raw_mm, 1)
                    if g >= 1:
                        turn(g - 1)
                turn(GROUPS - 1)

            def project_m(k):
                base = front_base(k) + GROUPS
                turn = turn_groups(base, lambda g, i: raw[:, g % 2, i:512:4])
                pe.wait_ge(z_sb, (k + 1) * TURNS)
                pe.wait_ge(init_sb, (k + 1) * 4)
                for g in range(GROUPS):
                    if g >= 2:
                        pe.wait_ge(raw_sb, base + g - 1)
                    for j in range(4):
                        o = 16 * g + 4 * j
                        last = mm(ps[32 * j:32 * j + 32, 4 + g % 2, :], proj_m[:], zt[:, :, o:o + 4],
                                  start=True, stop=True)
                    last.then_inc(raw_mm, 1)
                    if g >= 1:
                        turn(g - 1)
                turn(GROUPS - 1)

            def corr(k):
                def split_turn(q):
                    pe.wait_ge(low_set, k * CHUNKS + q + 1)
                    if q >= 1:
                        pe.wait_ge(split_sb, k * 2 * CHUNKS + 2 * q)
                    for o in range(QC):
                        last = tr(turned_parts[o // 8][:, o % 8, :], parts[q % 2][:, o, :, :].rearrange("p k r -> p (k r)"),
                                  ident_bf[:])
                    last.then_inc(split_mm, 1)

                def add_up(q):
                    for half in range(2):
                        if q >= 1:
                            pe.wait_ge(corr_add, k * 2 * CHUNKS + 2 * q - 1 + half)
                        if half == 0:
                            pe.wait_ge(split_sb, k * 2 * CHUNKS + 2 * q + 2)
                        for o in range(8 * half, 8 * half + 8):
                            area = ps[:, o // 4, P * (o % 4):P * (o % 4 + 1)]
                            mm(area, spread[:, o, :], waves_n[:], start=True, stop=False)
                            last = mm(area, waves_m[:], spread[:, o, :], start=False, stop=True)
                        last.then_inc(corr_mm, 1)

                pe.wait_ge(trn_sb, front_base(k) + 2 * GROUPS)
                pe.wait_ge(turn_read, k + 1)
                for q in range(CHUNKS):
                    split_turn(q)
                    add_up(q)

            def turn(k, t):
                for h in range(CH):
                    if t == 0:
                        if h == 0:
                            pe.wait_ge(corr_add, (k + 1) * 2 * CHUNKS)
                    else:
                        pe.wait_ge(out_add, k * TURNS + 2 * t - 1 + h)
                    for i in range(ROWS):
                        last = tr(ps[:, 2 + h, P * i:P * (i + 1)], zt[:, ROWS * t + i, P * h:P * (h + 1)], ident[:])
                    last.then_inc(turn_mm, 1)

            def mix(k, t):
                u = TILES + t
                pe.wait_ge(xin_in[u % XS], 16 * (k * ring_tiles + u // XS + 1))
                for pair in range(2):
                    if t >= 1:
                        pe.wait_ge(z_sb, k * TURNS + 2 * t - 1 + pair)
                    for i in range(2):
                        for h in range(CH):
                            row = 512 * h + P * (2 * pair + i)
                            last = mm(ps[:, pair, C * i:C * (i + 1)], xin[:, u % XS, row:row + P],
                                      wrt_sb[:, h, :], start=(h == 0), stop=(h == CH - 1))
                    last.then_inc(z_mm, 1)

            def small(k, t):
                if t == 0:
                    pe.wait_ge(trn_sb, front_base(k) + GROUPS)
                    for h in range(CH):
                        for r in range(NR):
                            last = mm(ps[:, 5, 49 * h + NR * r:49 * h + NR * (r + 1)], beta[:, r, P * h:P * (h + 1)],
                                      proj_n[:, 0:NR], start=True, stop=True)
                    last.then_inc(stat_mm, 1)
                if t < NR:
                    if t >= 1:
                        pe.wait_ge(bturn_sb, k * NR + t)
                    for h in range(CH):
                        last = tr(ps[:, 6, P * h:P * (h + 1)], beta[:, NR + t, P * h:P * (h + 1)], ident[:])
                    last.then_inc(bturn_mm, 1)
                if 1 <= t <= NR:
                    r = t - 1
                    pe.wait_ge(bturn_sb, k * NR + t)
                    if r >= 1:
                        pe.wait_ge(bmix_sb, k * NR + r)
                    for h in range(CH):
                        last = mm(ps[:, 4, 0:C], raw[:, r % 2, P * h:P * (h + 1)], wrt_sb[:, h, :],
                                  start=(h == 0), stop=(h == CH - 1))
                    last.then_inc(bmix_mm, 1)
                if t == 3:
                    pe.wait_ge(mag_set, k + 1)
                    for h in range(CH):
                        last = mm(ps[0:CENTRE_PAIRS, 5, 100:101], mag[:, h, :], mean[:],
                                  start=(h == 0), stop=(h == CH - 1))
                    last.then_inc(cen_mm, 1)
                if t == 4:
                    pe.wait_ge(cen_set, k + 1)
                    own_wait(pe)
                    mm(ps[0:32, 5, 104:105], w1a_sb[:], cen[:], start=True, stop=False)
                    mm(ps[0:32, 5, 104:105], w1b_sb[:], cen[0:CENTRE_PAIRS - 1, :],
                       start=False, stop=True).then_inc(hid_mm, 1)
                if t == 5:
                    pe.wait_ge(hid_set, k + 1)
                    mm(ps[:, 5, 108:111], hid_rep, w2_sb[:], start=True, stop=False)
                    mm(ps[:, 5, 108:111], ones[0:1, :], b2_sb[:], start=False, stop=True).then_inc(par_mm, 1)
                if t == 9:
                    pe.wait_ge(kern_set, k + 1)
                    for s in range(2):
                        mm(ps[:, 5, 128 + 8 * s:135 + 8 * s], trig[:, s, :], kern[0:KS, 56:63], start=True, stop=True)
                        mm(ps[:, 5, 144 + 8 * s:151 + 8 * s], trig[:, s, :], kern[0:KS, 49:56], start=True, stop=True)
                        last = mm(ps[0:KS, 5, 256 + P * s:256 + P * (s + 1)], kern[0:KS, 56:63], trig[:, s, :],
                                  start=True, stop=True)
                    last.then_inc(tab_mm, 1)
                if t == 10:
                    pe.wait_ge(tab_set, k + 1)
                    for s in range(2):
                        last = mm(ps[:, 5, 0:H], ptab[:, s, :], trig[:, s, :], start=(s == 0), stop=(s == 1))
                    last.then_inc(w_mm, 1)
                if t == 11:
                    pe.wait_ge(bmix_sb, (k + 1) * NR)
                    for h in range(CH):
                        for r in range(NR):
                            last = mm(ps[:, 7, 49 * h + NR * r:49 * h + NR * (r + 1)], gd[:, NR + r, P * h:P * (h + 1)],
                                      proj_m[:, 0:NR], start=True, stop=True)
                    last.then_inc(eps_mm, 1)
                if t == 12:
                    pe.wait_ge(eps_set, k + 1)
                    own_wait(pe)
                    for h in range(CH):
                        last = tr(ps[0:49, 7, 256 + P * h - 128:256 + P * h], eps_sb[:, h, :], ident[:])
                    last.then_inc(epst_mm, 1)
                if 16 <= t < 20:
                    i = t - 16
                    rows = range(2 * i, min(2 * i + 2, NR))
                    if i == 0:
                        pe.wait_ge(epst_set, k + 1)
                        pe.wait_ge(cmap_set, k + 1)
                    else:
                        pe.wait_ge(kap_sb, 4 * k + i)
                    own_wait(pe)
                    for r in rows:
                        last = mm(ps[0:NR, 6, C * (r % 2):C * (r % 2 + 1)], cmap[:, NR * r:NR * (r + 1)], eps_t,
                                  start=True, stop=True)
                    last.then_inc(kap_mm, 1)
                    pe.wait_ge(kap_sb, 4 * k + i + 1)
                    if i >= 1:
                        pe.wait_ge(init_sb, 4 * k + i)
                    mm(ps[:, 7, 0:C * len(rows)], nyq_t[:], raw[0:NR, i % 2, 0:C * len(rows)],
                       start=True, stop=True).then_inc(init_mm, 1)

            pe.wait_ge(const_in, CONST_READY)
            pe.wait_ge(const_set, 2)
            front(0)
            for t in range(TILES):
                mix(0, t)
                small(0, t)
            with pe.Fori(0, NB - 1) as k:
                project_m(k)
                front(k + 1)
                corr(k)
                for t in range(TILES):
                    turn(k, t)
                    mix(k + 1, t)
                    small(k + 1, t)
            project_m(NB - 1)
            corr(NB - 1)
            for t in range(TILES):
                turn(NB - 1, t)

        @block_ctx.scalar
        def _(act):
            def copy(o, i):
                return nc.scalar.activation(o, i, ACT.Copy)

            def evacuate(base, rows, dst):
                def turned(g):
                    act.wait_ge(trn_mm, base + g + 1)
                    copy(dst[:, :, 16 * g:16 * g + 16].rearrange("p r (j i) -> p r j i", j=4),
                         ps[:, 6 + g % 2, :].rearrange("p (i j r) -> p r j i", i=4, j=4)[:, 0:rows, :, :])\
                        .then_inc(trn_sb, 1)
                for g in range(GROUPS):
                    act.wait_ge(raw_mm, base + g + 1)
                    if g >= 2:
                        act.wait_ge(trn_mm, base + g - 1)
                    copy(raw[:, g % 2, :], ps[:, 4 + g % 2, :]).then_inc(raw_sb, 1)
                    if g >= 1:
                        turned(g - 1)
                turned(GROUPS - 1)

            def front(k):
                evacuate(front_base(k), 2 * NR, beta[:, :, :])

            def project_m(k):
                act.wait_ge(dproj_free, k + 1)
                evacuate(front_base(k) + GROUPS, NR, dproj[:, :, :])

            def corr(k):
                gv = gd[:, :, :].rearrange("p r o -> p o r")

                def lead(q):
                    if q >= 2:
                        act.wait_ge(split_mm, k * CHUNKS + q - 1)
                    src = gv[:, QC * q:QC * (q + 1), :].unsqueeze(2).broadcast_to([P, QC, 3, 2 * NR])
                    copy(parts[q % 2][:, :, 0:3, :], src).then_inc(lead_set, 1)

                def middle(q):
                    act.wait_ge(rest_set, k * CHUNKS + q + 1)
                    src = rest[:, q % 2, :, :].unsqueeze(2).broadcast_to([P, QC, 2, 2 * NR])
                    copy(parts[q % 2][:, :, 3:5, :], src).then_inc(mid_set, 1)

                def turned(q):
                    act.wait_ge(split_mm, k * CHUNKS + q + 1)
                    if q >= 1:
                        act.wait_ge(corr_mm, (k * CHUNKS + q) * 2)
                    for i in range(2):
                        copy(spread[:, 8 * i:8 * i + 8, :], turned_parts[i]).then_inc(split_sb, 1)

                act.wait_ge(gamma_done, k + 1)
                act.wait_ge(delta_done, k + 1)
                act.wait_ge(shared_free, k + 1)
                lead(0)
                middle(0)
                for q in range(CHUNKS):
                    if q + 1 < CHUNKS:
                        lead(q + 1)
                        middle(q + 1)
                    turned(q)

            def z_rows(k, t):
                for pair in range(2):
                    act.wait_ge(z_mm, k * TURNS + 2 * t + pair + 1)
                    n = ROWS * t + 2 * pair
                    copy(zt[:, n:n + 2, :], ps[:, pair, :].rearrange("p (n o) -> p n o", n=2)).then_inc(z_sb, 1)

            def small(k, t):
                if t < NR:
                    act.wait_ge(bturn_mm, k * NR + t + 1)
                    if t >= 2:
                        act.wait_ge(bmix_mm, k * NR + t - 1)
                    copy(raw[:, t % 2, 0:C], ps[:, 6, 0:C]).then_inc(bturn_sb, 1)
                if 1 <= t <= NR:
                    act.wait_ge(bmix_mm, k * NR + t)
                    copy(gd[:, NR + t - 1, :], ps[:, 4, 0:C]).then_inc(bmix_sb, 1)
                if t == 2:
                    act.wait_ge(stat_sq, k + 1)
                    nc.scalar.activation(mag, re, ACT.Sqrt).then_inc(mag_set, 1)
                if t == 5:
                    act.wait_ge(rsq_set, k + 1)
                    nc.scalar.activation(pc[:, 14:15], pc[:, 13:14], ACT.Sqrt).then_inc(rad_set, 1)
                if t == 6:
                    act.wait_ge(hsq_set, k + 1)
                    nc.scalar.activation(pc[:, 20:21], pc[:, 19:20], ACT.Sqrt).then_inc(half_set, 1)
                    nc.scalar.activation(pc[:, 27:28], pc[:, 2:3], ACT.Exp).then_inc(lam_set, 1)
                if t == 7:
                    act.wait_ge(expo_set, k + 1)
                    nc.scalar.activation(g4, g3, ACT.Exp, scale=-1.0).then_inc(exp_set, 1)
                if t == 10:
                    act.wait_ge(w_mm, k + 1)
                    copy(wt[:], ps[:, 5, 0:H]).then_inc(w_set, 1)
                if t == 12:
                    act.wait_ge(epst_mm, k + 1)
                    copy(eps_t, ps[0:49, 7, 128:384]).then_inc(epst_set, 1)
                if 16 <= t < 20:
                    i = t - 16
                    nr = len(range(2 * i, min(2 * i + 2, NR)))
                    act.wait_ge(kap_mm, 4 * k + i + 1)
                    if i >= 2:
                        act.wait_ge(init_mm, 4 * k + i - 1)
                    copy(raw[0:NR, i % 2, 0:C * nr], ps[0:NR, 6, 0:C * nr]).then_inc(kap_sb, 1)
                    act.wait_ge(init_mm, 4 * k + i + 1)
                    copy(gd[:, 2 * i:2 * i + nr, :], ps[:, 7, 0:C * nr].rearrange("p (r o) -> p r o", r=nr))\
                        .then_inc(init_sb, 1)

            front(0)
            for t in range(TILES):
                z_rows(0, t)
                small(0, t)
            with act.Fori(0, NB - 1) as k:
                project_m(k)
                front(k + 1)
                corr(k)
                for t in range(TILES):
                    z_rows(k + 1, t)
                    small(k + 1, t)
            project_m(NB - 1)
            corr(NB - 1)

        @block_ctx.vector
        def _(dve):
            ts, tt = nc.vector.tensor_scalar, nc.vector.tensor_tensor
            stt, cp = nc.vector.scalar_tensor_tensor, nc.vector.tensor_copy
            step = [0]

            def restart():
                dve.sem_clear(dve_step)
                step[0] = 0

            def mark(ins):
                step[0] += 1
                ins.then_inc(dve_step, 1)

            def settle():
                dve.wait_ge(dve_step, step[0])

            def link(ins):
                mark(ins)
                settle()

            nc.vector.memset(ones[:], 1.0).then_inc(const_set, 1)
            nc.vector.memset(mean[:], 1.0 / (P * C)).then_inc(const_set, 1)
            dve.wait_ge(const_in, CONST_READY)
            dve.wait_ge(const_set, 2)

            def col(i, j=None):
                return pc[:, i:(i + 1 if j is None else j)]

            def spectrum(k):
                dve.wait_ge(stat_mm, k + 1)
                link(cp(spec, ps[:, 5, 0:98].rearrange("p (h f) -> p h f", h=CH)))
                v = spec.rearrange("p h (r s) -> p h r s", r=NR)
                c_, s_ = slice(1, NR, 2), slice(2, NR, 2)
                cc, ss, cs, sc = v[:, :, c_, c_], v[:, :, s_, s_], v[:, :, c_, s_], v[:, :, s_, c_]

                def grid_of(t, side):
                    a = t[:, :, 3:24].rearrange("p h (a b) -> p h a b", a=R)
                    return a[:, :, :, 4:7] if side > 0 else a[:, :, :, 2::-1]
                mark(nc.vector.memset(im[:, :, 24:25], 0.0))
                mark(cp(re[:, :, 24:25], v[:, :, 0, 0:1]))
                mark(cp(re[:, :, 0:3], v[:, :, 0, c_]))
                mark(cp(im[:, :, 0:3], v[:, :, 0, s_]))
                mark(cp(re[:, :, 6:24:7], v[:, :, c_, 0]))
                mark(cp(im[:, :, 6:24:7], v[:, :, s_, 0]))
                mark(tt(grid_of(re, 1), cc, ss, ALU.subtract))
                mark(tt(grid_of(re, -1), cc, ss, ALU.add))
                mark(tt(grid_of(im, 1), cs, sc, ALU.add))
                mark(tt(grid_of(im, -1), cs, sc, ALU.subtract))
                settle()
                mark(tt(re, re, re, ALU.mult))
                mark(tt(im[:, :, 0:24], im[:, :, 0:24], im[:, :, 0:24], ALU.mult))
                settle()
                tt(re, re, im, ALU.add).then_inc(stat_sq, 1)

            def centre(k):
                dve.wait_ge(cen_mm, k + 1)
                cp(cen[:], ps[0:CENTRE_PAIRS, 5, 100:101]).then_inc(cen_set, 1)

            def hidden(k):
                dve.wait_ge(hid_mm, k + 1)
                link(ts(hid[:], ps[0:32, 5, 104:105], b1_sb[:], 0.0, ALU.add, ALU.max))
                ts(hid_rep, ones[:], hid[:], None, ALU.mult).then_inc(hid_set, 1)

            def direction(k):
                dve.wait_ge(par_mm, k + 1)
                link(cp(col(0, 3), ps[:, 5, 108:111]))
                link(stt(col(3, 5), col(0, 2), -1.0, col(0, 2), ALU.mult, ALU.max))
                link(tt(col(5), col(3), col(4), ALU.max))
                link(ts(col(6), col(5), 0.0, None, ALU.is_equal))
                link(tt(col(7), col(5), col(6), ALU.add))
                link(nc.vector.reciprocal(col(8), col(7)))
                link(ts(col(9, 11), col(0, 2), col(8), None, ALU.mult))
                link(tt(col(10), col(10), col(6), ALU.add))
                link(tt(col(11, 13), col(9, 11), col(9, 11), ALU.mult))
                tt(col(13), col(11), col(12), ALU.add).then_inc(rsq_set, 1)

            def half_angle(k):
                dve.wait_ge(rad_set, k + 1)
                link(nc.vector.reciprocal(col(15), col(14)))
                link(ts(col(16, 18), col(9, 11), col(15), None, ALU.mult))
                link(stt(col(18), col(17), -1.0, col(17), ALU.mult, ALU.max))
                ts(col(19), col(18), 0.5, 0.5, ALU.mult, ALU.add).then_inc(hsq_set, 1)

            def exponents(k):
                dve.wait_ge(half_set, k + 1)
                dve.wait_ge(lam_set, k + 1)
                link(nc.vector.reciprocal(col(21), col(20)))
                link(stt(col(22), col(16), 0.5, col(21), ALU.mult, ALU.mult))
                mark(ts(col(23), col(17), 0.0, None, ALU.is_ge))
                mark(tt(col(24), col(20), col(22), ALU.subtract))
                mark(tt(col(28), col(27), col(27), ALU.mult))
                mark(ts(col(30), col(27), EPS, None, ALU.add))
                settle()
                mark(stt(col(25), col(24), col(23), col(22), ALU.mult, ALU.add))
                mark(stt(col(26), col(24), col(23), col(20), ALU.mult, ALU.subtract))
                mark(ts(col(28), col(28), 2.0, None, ALU.mult))
                mark(nc.vector.reciprocal(col(31), col(30)))
                settle()
                mark(nc.vector.reciprocal(col(29), col(28)))
                mark(tt(col(32), col(31), col(31), ALU.mult))
                mark(ts(g1, grid[:, 1, :], col(25), None, ALU.mult))
                mark(ts(g2, grid[:, 0, :], col(25), None, ALU.mult))
                settle()
                mark(ts(col(32), col(32), 2.0, None, ALU.mult))
                mark(stt(g3, grid[:, 0, :], col(26), g1, ALU.mult, ALU.add))
                mark(stt(g4, grid[:, 1, :], col(26), g2, ALU.mult, ALU.subtract))
                settle()
                mark(nc.vector.reciprocal(col(33), col(32)))
                mark(tt(g1, g3, g3, ALU.mult))
                mark(tt(g2, g4, g4, ALU.mult))
                settle()
                link(ts(g2, g2, col(33), None, ALU.mult))
                stt(g3, g1, col(29), g2, ALU.mult, ALU.add).then_inc(expo_set, 1)

            def normalise(k):
                dve.wait_ge(exp_set, k + 1)
                link(nc.vector.tensor_reduce(col(34), g4[:, 0:49], AX.X, ALU.add))
                link(ts(col(35), col(34), EPS, None, ALU.add))
                link(nc.vector.reciprocal(col(36), col(35)))
                ts(kern, g4, col(36), None, ALU.mult).then_inc(kern_set, 1)
                dve.wait_ge(kern_set, k + 1)

            def corner_map(k):
                for i, (a, b) in enumerate(CORNER_PAIRS):
                    kv = kern[0:49, KS * a + b:KS * a + b + 1]
                    if i == 0:
                        link(ts(cmap, corner[:, 0, :], kv, None, ALU.mult))
                    elif i < len(CORNER_PAIRS) - 1:
                        link(stt(cmap, corner[:, i, :], kv, cmap, ALU.mult, ALU.add))
                    else:
                        stt(cmap, corner[:, i, :], kv, cmap, ALU.mult, ALU.add).then_inc(cmap_set, 1)

            def scale_tables(k):
                dve.wait_ge(tab_mm, k + 1)
                for axis in range(2):
                    src = ps[:, 5, 128 + 16 * axis:144 + 16 * axis].rearrange("p (t d) -> p t d", t=2)[:, :, 4:7]
                    for i, s in enumerate(SCALES):
                        mark(ts(kn[:, axis, i, :].rearrange("p (t d) -> p t d", t=2), src, s / P, None, ALU.mult))
                mark(cp(ptab[:, 0, :], ps[0:KS, 5, 256:384]))
                mark(ts(ptab[:, 1, :], ps[0:KS, 5, 384:512], -1.0, None, ALU.mult))
                settle()
                dve.sem_inc(tab_set, 1)

            def eps_copy(k):
                dve.wait_ge(eps_mm, k + 1)
                cp(eps_sb, ps[:, 7, 0:98].rearrange("p (h f) -> p h f", h=CH)).then_inc(eps_set, 1)

            def multiply_rows(axis, src, dst_row, fresh):
                seen = set()
                for rnd in ROUNDS:
                    for row, s, part, j, p in rnd:
                        kv = kn[:, axis, SCALES.index(-s), 3 * part + j - 1:3 * part + j]
                        dst = gd[:, dst_row + row, :]
                        if fresh and row not in seen:
                            mark(ts(dst, src(p), kv, None, ALU.mult))
                        else:
                            mark(stt(dst, src(p), kv, dst, ALU.mult, ALU.add))
                        seen.add(row)
                    settle()

            def gamma(k):
                dve.wait_ge(init_sb, 4 * k + 4)
                multiply_rows(0, lambda p: gd[:, NR + p, :], 0, False)
                dve.sem_inc(gamma_done, 1)

            def delta(k):
                dve.wait_ge(trn_sb, front_base(k) + 2 * GROUPS)
                multiply_rows(1, lambda p: dproj[:, p, :], NR, True)
                dve.sem_inc(delta_done, 1)
                dve.sem_inc(dproj_free, 1)

            def window(k):
                restart()
                dve.wait_ge(w_set, k + 1)
                dve.wait_ge(raw_mm, front_base(k) + 2 * GROUPS)
                for n in range(0, H, 16):
                    v = zt[:, n:n + 16, :]
                    mark(tt(v, v, wt[:, n:n + 16].unsqueeze(2).broadcast_to([P, 16, C]), ALU.mult))
                delta(k)
                settle()

            def corr(k):
                restart()

                def split(q):
                    dve.wait_ge(lead_set, k * CHUNKS + q + 1)
                    if q >= 2:
                        dve.wait_ge(mid_set, k * CHUNKS + q - 1)
                    gv = gd[:, :, QC * q:QC * (q + 1)].rearrange("p r o -> p o r")
                    tt(rest[:, q % 2, :, :], gv, parts[q % 2][:, :, 0, :], ALU.subtract).then_inc(rest_set, 1)
                    dve.wait_ge(rest_set, k * CHUNKS + q + 1)
                    dve.wait_ge(mid_set, k * CHUNKS + q + 1)
                    tt(parts[q % 2][:, :, 5, :], rest[:, q % 2, :, :], parts[q % 2][:, :, 3, :],
                       ALU.subtract).then_inc(low_set, 1)

                split(0)
                for q in range(CHUNKS):
                    if q + 1 < CHUNKS:
                        split(q + 1)
                    for half in range(2):
                        dve.wait_ge(corr_mm, (k * CHUNKS + q) * 2 + half + 1)
                        o = QC * q + 8 * half
                        v = zt[:, :, o:o + 8].rearrange("p n o -> p o n")
                        tt(v, v, ps[:, 2 * half:2 * half + 2, :].rearrange("p b (o n) -> p (b o) n", n=H),
                           ALU.add).then_inc(corr_add, 1)

            def out_rows(k, t):
                dve.wait_ge(xres_in[t % OS], 16 * (k * slot_tiles[t % OS] + t // OS + 1))
                for h in range(CH):
                    dve.wait_ge(turn_mm, k * TURNS + 2 * t + h + 1)
                    v = xo[:, t % OS, 512 * h:512 * (h + 1)]
                    tt(v, v, ps[:, 2 + h, :], ALU.add).then_inc(out_add, 1)

            def small(k, t):
                for at, work in ((1, spectrum), (3, centre), (4, hidden), (5, direction), (6, half_angle),
                                 (7, exponents), (8, normalise), (8, corner_map), (9, scale_tables),
                                 (11, eps_copy), (20, gamma)):
                    if t == at:
                        work(k)

            dve.sem_inc(dproj_free, 1)
            dve.sem_inc(turn_read, 1)
            restart()
            for t in range(TILES):
                small(0, t)
            with dve.Fori(0, NB - 1) as k:
                window(k)
                corr(k)
                restart()
                for t in range(TILES):
                    out_rows(k, t)
                    small(k + 1, t)
                dve.wait_ge(out_add, (k + 1) * TURNS)
                dve.sem_inc(turn_read, 1)
            window(NB - 1)
            corr(NB - 1)
            for t in range(TILES):
                out_rows(NB - 1, t)


def kernel(x, L0_conv_w1, L0_conv_b1, L0_conv_w2, L0_conv_b2, L0_conv_wr):
    import concourse.bacc as bacc
    from concourse.bass_utils import run_bass_kernel_spmd

    x = np.ascontiguousarray(x)
    w1 = np.asarray(L0_conv_w1)
    mid = 24
    arrays = {
        "x": x,
        "w1a": np.ascontiguousarray(np.concatenate([w1[mid + 1:], w1[mid:mid + 1]])),
        "w1b": np.ascontiguousarray(w1[mid - 1::-1]),
        "b1": np.ascontiguousarray(np.asarray(L0_conv_b1).reshape(32, 1)),
        "w2": np.ascontiguousarray(L0_conv_w2),
        "b2": np.ascontiguousarray(np.asarray(L0_conv_b2).reshape(1, 3)),
        "wrt": np.ascontiguousarray(np.asarray(L0_conv_wr).T.reshape(CH, P, C).transpose(1, 0, 2)),
    }
    arrays.update(tables())
    nc = bacc.Bacc("TRN2", target_bir_lowering=False, num_devices=1)
    aps = {n: nc.dram_tensor(f"in_{n}", a.shape, mybir.dt.from_np(a.dtype), kind="ExternalInput").ap()
           for n, a in arrays.items()}
    out = nc.dram_tensor("out", (NB, C, H, W), F32, kind="ExternalOutput").ap()
    own = {n: aps[n] for n in ("x", "w1a", "w1b", "b1", "w2", "b2", "wrt")}
    tab = {n: a for n, a in aps.items() if n not in own}
    build(nc, **own, tab=tab, out=out)
    r = run_bass_kernel_spmd(nc, [{f"in_{n}": a for n, a in arrays.items()}], core_ids=[0])
    return r.results[0]["out"]
```

```python
from contextlib import ExitStack

import numpy as np

import concourse.bass as bass
from concourse import mybir

F32 = mybir.dt.float32
BF16 = mybir.dt.bfloat16
ALU = mybir.AluOpType
ACT = mybir.ActivationFunctionType
AX = mybir.AxisListType

P = 128
NB, C, H, W = 8, 256, 128, 128
KS = 7
R = 3
EPS = 1e-8
TH = 2.0 * np.pi / 128
CH = C // P
NR = 7
GROUPS = 16
TILES = 32
ROWS = H // TILES
XS = 4
OS = 3
QC = 16
HC = QC // 2
CHUNKS = C // QC
EARLY_FRONT = 4
EARLY_ROWS = 10
REPS = 6
KROWS = REPS * 2 * NR
PARTS = [(0, 0), (0, 1), (0, 2), (1, 0), (1, 1), (2, 0)]
CENTRE_PAIRS = 25
TERMS = [(0, 1, 0, 1, 1), (0, -1, 1, 1, 2), (0, 1, 0, 2, 3), (0, -1, 1, 2, 4), (0, 1, 0, 3, 5), (0, -1, 1, 3, 6),
         (1, 1, 0, 1, 0), (1, 2, 0, 2, 1), (1, -2, 1, 2, 2), (1, 2, 0, 3, 3), (1, -2, 1, 3, 4),
         (2, -1, 1, 1, 0), (2, -2, 0, 2, 2), (2, -2, 1, 2, 1), (2, -2, 0, 3, 4), (2, -2, 1, 3, 3),
         (3, 1, 0, 2, 0), (3, 2, 0, 3, 1), (3, -2, 1, 3, 2),
         (4, -1, 1, 2, 0), (4, -2, 0, 3, 2), (4, -2, 1, 3, 1),
         (5, 1, 0, 3, 0), (6, -1, 1, 3, 0)]
SCALES = [-1, 1, -2, 2]


def term_rounds():
    rounds, left = [], list(TERMS)
    while left:
        seen, now = set(), []
        for t in list(left):
            if t[0] not in seen:
                seen.add(t[0])
                now.append(t)
                left.remove(t)
        rounds.append(now)
    return rounds


ROUNDS = term_rounds()


def waves(sign):
    n = np.arange(P)
    s = np.where(n % 2 == 1, float(sign), 1.0)
    cols = [s]
    for q in range(1, R + 1):
        cols += [s * np.cos(TH * q * n), s * np.sin(TH * q * n)]
    return np.stack(cols, 1)


def wrapped():
    v = np.zeros((KS, NR, NR), complex)

    def wave(q, s):
        u = np.zeros(NR, complex)
        if q == 0:
            u[0] = 1
        else:
            u[2 * abs(q) - 1] = 1
            u[2 * abs(q)] = s * 1j * np.sign(q)
        return u

    for j in range(-R, R + 1):
        for q in range(-R, R + 1):
            src = q + j
            if -R <= src <= R and ((j > 0 and q < 0 <= src) or (j < 0 and q >= 0 > src)):
                v[j + R] += np.outer(wave(q, 1), wave(src, -1)) / P
    return v


CORNER_PAIRS = [(a, b) for a in range(R + 1, KS) for b in range(KS) if b != R]


def bf16_bits(a):
    bits = a.astype(np.float32).view(np.uint32).astype(np.uint64)
    return ((bits + 0x7FFF + ((bits >> 16) & 1)) >> 16).astype(np.uint16)


def bf16_parts(a):
    parts, rest = [], a.astype(np.float64)
    for _ in range(3):
        p = (bf16_bits(rest).astype(np.uint32) << 16).view(np.float32).astype(np.float64)
        parts.append(p)
        rest = rest - p
    return parts


def tables():
    low, nyq = waves(1), waves(-1)
    m, d = np.arange(P), np.arange(-R, R + 1)
    proj_n = np.zeros((P, 32))
    proj_n[:, 0:NR], proj_n[:, NR:2 * NR] = low, nyq
    proj_m = np.zeros((P, 32))
    proj_m[:, 0:NR] = nyq
    trig = np.stack([np.cos(TH * np.outer(d, m)), np.sin(TH * np.outer(d, m))], 1)
    xx, yy = np.zeros((P, 63)), np.zeros((P, 63))
    f = np.arange(49)
    xx[:, :49], yy[:, :49] = f % KS - R, f // KS - R
    xx[:KS, 49:56], yy[:KS, 49:56] = d[None, :], d[:, None]
    xx[:KS, 56:63], yy[:KS, 56:63] = d[:, None], d[None, :]
    v = wrapped()
    corner = np.zeros((49, len(CORNER_PAIRS), 49))
    for i, (a, b) in enumerate(CORNER_PAIRS):
        for aa, bb in ((a, b), (KS - 1 - a, KS - 1 - b)):
            t = np.einsum("rp,sq->pqrs", v[aa], v[bb]).real
            corner[:, i, :] += t.reshape(49, 49)
    e = [p.T for p in bf16_parts(nyq)]
    waves_n = np.zeros((REPS, 2, NR, P))
    waves_m = np.zeros((REPS, 2, NR, P))
    for i, (_, part) in enumerate(PARTS):
        waves_n[i, 0] = e[part]
        waves_m[i, 1] = e[part]
    waves_n, waves_m = waves_n.reshape(KROWS, P), waves_m.reshape(KROWS, P)
    f32 = lambda a: np.ascontiguousarray(a.astype(np.float32))
    bf = lambda a: np.ascontiguousarray(bf16_bits(a))
    return {
        "proj_n": f32(proj_n), "proj_m": f32(proj_m), "nyq_t": f32(nyq.T), "trig": f32(trig),
        "grid": f32(np.stack([xx, yy], 1)), "corner": f32(corner), "ident": f32(np.eye(P)),
        "ident_bf": bf(np.eye(P)), "waves_n": bf(waves_n), "waves_m": bf(waves_m),
    }


def build(nc, x, w1a, w1b, b1, w2, b2, wrt, tab, out):
    with ExitStack() as ctx:
        def sb(name, shape, dt=F32):
            return ctx.enter_context(nc.sbuf_tensor(name, shape, dt))

        def sem(name):
            return ctx.enter_context(nc.semaphore(name))

        zt = sb("zt", [P, H, C])
        xin = sb("xin", [P, XS, 1024])
        shared = sb("shared", [P, OS * 1024])
        xo = shared[:, :].rearrange("p (s f) -> p s f", s=OS)
        parts = [shared[:, i * 672:(i + 1) * 672].bitcast(BF16).rearrange("p (o k r) -> p o k r", o=QC, k=REPS)
                 for i in range(2)]
        spread = shared[0:KROWS, 1344:2368].bitcast(BF16).rearrange("p (o f) -> p o f", o=QC)
        rest = shared[:, 2368:2816].rearrange("p (s o r) -> p s o r", s=2, o=QC)
        beta = sb("beta", [P, 2 * NR, C])
        gd = sb("gd", [P, 2 * NR, C])
        dproj = sb("dproj", [P, NR, C])
        raw = sb("raw", [P, 2, 512])
        proj_n = sb("proj_n_sb", [P, 32])
        proj_m = sb("proj_m_sb", [P, 32])
        nyq_t = sb("nyq_t_sb", [NR, P])
        trig = sb("trig_sb", [KS, 2, P])
        grid = sb("grid_sb", [P, 2, 63])
        corner = sb("corner_sb", [49, len(CORNER_PAIRS), 49])
        ident = sb("ident_sb", [P, P])
        ident_bf = sb("ident_bf_sb", [P, P], BF16)
        waves_n = sb("waves_n_sb", [KROWS, P], BF16)
        waves_m = sb("waves_m_sb", [KROWS, P], BF16)
        wrt_sb = sb("wrt_sb", [P, CH, C])
        w1a_sb = sb("w1a_sb", [CENTRE_PAIRS, 32])
        w1b_sb = sb("w1b_sb", [CENTRE_PAIRS - 1, 32])
        b1_sb = sb("b1_sb", [32, 1])
        w2_sb = sb("w2_sb", [32, 3])
        b2_sb = sb("b2_sb", [1, 3])
        ones = sb("ones", [32, P])
        mean = sb("mean", [P, 1])
        pc = sb("pc", [P, 40])
        kn = sb("kn", [P, 2, len(SCALES), 6])
        wt = sb("wt", [P, H])
        cen = sb("cen", [CENTRE_PAIRS, 1])
        hid = sb("hid", [32, 1])
        flat = dproj[:, :, :].rearrange("p r o -> p (r o)")
        taken = [0]

        def scratch(rows, n):
            taken[0] += n
            assert taken[0] <= NR * C
            return flat[0:rows, taken[0] - n:taken[0]]

        spec = scratch(P, CH * 49).rearrange("p (h f) -> p h f", h=CH)
        re = scratch(P, CH * CENTRE_PAIRS).rearrange("p (h f) -> p h f", h=CH)
        im = scratch(P, CH * CENTRE_PAIRS).rearrange("p (h f) -> p h f", h=CH)
        mag = scratch(P, CH * CENTRE_PAIRS).rearrange("p (h f) -> p h f", h=CH)
        hid_rep = scratch(32, P)
        g1, g2, g3, g4 = (scratch(P, 63) for _ in range(4))
        kern = scratch(P, 63)
        ptab = scratch(KS, 2 * P).rearrange("p (t m) -> p t m", t=2)
        cmap = scratch(49, 49)
        eps_sb = scratch(P, CH * 49).rearrange("p (h f) -> p h f", h=CH)
        eps_t = scratch(49, C)

        ps = ctx.enter_context(nc.psum_tensor("ps", [P, 8, 512], F32))
        turned_parts = [ps[0:KROWS, 4 + i, :].bitcast(BF16).rearrange("p (o f) -> p o f", o=QC // 2) for i in range(2)]

        const_in = sem("const_in")
        const_set = sem("const_set")
        xin_in = [sem(f"xin_in{i}") for i in range(XS)]
        xres_in = [sem(f"xres_in{i}") for i in range(OS)]
        stored = [sem(f"stored{i}") for i in range(OS)]
        raw_mm, raw_sb, trn_mm, trn_sb = sem("raw_mm"), sem("raw_sb"), sem("trn_mm"), sem("trn_sb")
        z_mm, z_sb = sem("z_mm"), sem("z_sb")
        turn_mm, out_add = sem("turn_mm"), sem("out_add")
        wz_done = sem("wz_done")
        delta_done = sem("delta_done")
        gamma_done = sem("gamma_done")
        lead_set, rest_set, mid_set, low_set = sem("lead_set"), sem("rest_set"), sem("mid_set"), sem("low_set")
        split_mm, split_sb = sem("split_mm"), sem("split_sb")
        corr_mm, corr_add = sem("corr_mm"), sem("corr_add")
        bturn_mm, bturn_sb, bmix_mm, bmix_sb = sem("bturn_mm"), sem("bturn_sb"), sem("bmix_mm"), sem("bmix_sb")
        stat_mm, stat_sq, mag_set = sem("stat_mm"), sem("stat_sq"), sem("mag_set")
        cen_mm, cen_set, hid_mm, hid_set, par_mm = sem("cen_mm"), sem("cen_set"), sem("hid_mm"), sem("hid_set"), sem("par_mm")
        rsq_set, rad_set, hsq_set, half_set, lam_set = (sem("rsq_set"), sem("rad_set"), sem("hsq_set"),
                                                        sem("half_set"), sem("lam_set"))
        expo_set, exp_set, kern_set = sem("expo_set"), sem("exp_set"), sem("kern_set")
        tab_mm, tab_set, w_mm, w_set = sem("tab_mm"), sem("tab_set"), sem("w_mm"), sem("w_set")
        eps_mm, eps_set, epst_mm, epst_set, cmap_set = (sem("eps_mm"), sem("eps_set"), sem("epst_mm"),
                                                        sem("epst_set"), sem("cmap_set"))
        kap_mm, kap_sb, init_mm, init_sb = sem("kap_mm"), sem("kap_sb"), sem("init_mm"), sem("init_sb")
        dve_step = sem("dve_step")

        shared_free = sem("shared_free")
        turn_read = sem("turn_read")
        dproj_free = sem("dproj_free")
        passed = sem("passed")

        consts = [(proj_n, tab["proj_n"]), (proj_m, tab["proj_m"]), (nyq_t, tab["nyq_t"]), (trig, tab["trig"]),
                  (grid, tab["grid"]), (corner, tab["corner"]), (ident, tab["ident"]),
                  (ident_bf, tab["ident_bf"].bitcast(BF16)), (waves_n, tab["waves_n"].bitcast(BF16)),
                  (waves_m, tab["waves_m"].bitcast(BF16)), (wrt_sb, wrt),
                  (w1a_sb, w1a), (w1b_sb, w1b), (b1_sb, b1), (w2_sb, w2), (b2_sb, b2)]
        CONST_READY = 16 * len(consts)

        TURNS = 2 * TILES
        slot_tiles = [len(range(s, TILES, OS)) for s in range(OS)]
        ring_tiles = 2 * TILES // XS

        def front_base(k):
            return k * (2 * GROUPS)

        block_ctx = ctx.enter_context(nc.Block())

        def own_wait(engine):
            engine.sem_inc(passed, 1)

        @block_ctx.sync
        def _(sp):
            for dst, src in consts:
                sp.dma_start(dst[:], src).then_inc(const_in, 16)

            def front_load(k, first):
                for u in range(TILES):
                    if u >= XS:
                        sp.wait_ge(raw_mm, front_base(k) + (u - XS) // 2 + 1)
                    elif not first:
                        sp.wait_ge(z_mm, k * TURNS - 2 * (XS - u) + 2)
                    sp.dma_start(xin[:, u % XS, :].rearrange("p (c m) -> p c m", c=8),
                                 x[k, 8 * u:8 * u + 8, :, :].rearrange("c n m -> n c m")).then_inc(xin_in[u % XS], 16)

            def mix_load(k):
                for t in range(TILES):
                    if t >= XS:
                        sp.wait_ge(z_mm, k * TURNS + 2 * (t - XS) + 2)
                    else:
                        sp.wait_ge(raw_mm, front_base(k) + (TILES + t - XS) // 2 + 1)
                    sp.dma_start(xin[:, t % XS, :].rearrange("p (h f) -> p h f", h=CH),
                                 x[k, :, ROWS * t:ROWS * (t + 1), :].rearrange("(h c) n m -> c h (n m)", h=CH))\
                      .then_inc(xin_in[t % XS], 16)

            front_load(0, True)
            mix_load(0)
            with sp.Fori(0, NB - 1) as k:
                front_load(k + 1, False)
                mix_load(k + 1)

        @block_ctx.gpsimd
        def _(pool):
            def store(k, t):
                pool.wait_ge(out_add, k * TURNS + 2 * t + 2)
                own_wait(pool)
                pool.dma_start(out[k, :, ROWS * t:ROWS * (t + 1), :].rearrange("(h c) n m -> c h (n m)", h=CH),
                               xo[:, t % OS, :].rearrange("p (h f) -> p h f", h=CH)).then_inc(stored[t % OS], 16)

            def turn_io(k):
                pool.wait_ge(corr_mm, (k + 1) * 2 * CHUNKS)
                for t in range(TILES):
                    if t >= OS:
                        pool.wait_ge(stored[t % OS], 16 * (k * slot_tiles[t % OS] + t // OS))
                    own_wait(pool)
                    pool.dma_start(xo[:, t % OS, :].rearrange("p (h f) -> p h f", h=CH),
                                   x[k, :, ROWS * t:ROWS * (t + 1), :].rearrange("(h c) n m -> c h (n m)", h=CH))\
                        .then_inc(xres_in[t % OS], 16)
                    if t >= 1:
                        store(k, t - 1)
                store(k, TILES - 1)
                for s in range(OS):
                    pool.wait_ge(stored[s], 16 * (k + 1) * slot_tiles[s])
                pool.sem_inc(shared_free, 1)

            pool.sem_inc(shared_free, 1)
            with pool.Fori(0, NB - 1) as k:
                turn_io(k)
            turn_io(NB - 1)
            for s in range(OS):
                pool.wait_ge(stored[s], 16 * NB * slot_tiles[s])

        @block_ctx.tensor
        def _(pe):
            mm = nc.tensor.matmul
            tr = nc.tensor.transpose

            def front_project(k, g):
                if g >= 1:
                    pe.wait_ge(raw_sb, front_base(k) + g)
                for j in range(4):
                    u = 2 * g + j // 2
                    if j % 2 == 0:
                        pe.wait_ge(xin_in[u % XS], 16 * (k * ring_tiles + u // XS + 1))
                    last = mm(ps[32 * j:32 * j + 32, 6, :], proj_n[:],
                              xin[:, u % XS, 512 * (j % 2):512 * (j % 2) + 512], start=True, stop=True)
                last.then_inc(raw_mm, 1)

            def front_turn(k, g):
                pe.wait_ge(raw_sb, front_base(k) + g + 1)
                if g >= 1:
                    pe.wait_ge(trn_sb, front_base(k) + g)
                for i in range(4):
                    last = tr(ps[:, 7, P * i:P * (i + 1)], raw[:, g % 2, P * i:P * (i + 1)], ident[:])
                last.then_inc(trn_mm, 1)

            def project_m(k):
                base = front_base(k) + GROUPS

                def turn(g):
                    pe.wait_ge(raw_sb, base + g + 1)
                    if g >= 2:
                        pe.wait_ge(trn_sb, base + g - 1)
                    for i in range(4):
                        last = tr(ps[:, g % 2, P * i:P * (i + 1)], raw[:, g % 2, i:512:4], ident[:])
                    last.then_inc(trn_mm, 1)

                pe.wait_ge(z_sb, (k + 1) * TURNS)
                pe.wait_ge(init_sb, (k + 1) * 4)
                for g in range(GROUPS):
                    if g >= 2:
                        pe.wait_ge(raw_sb, base + g - 1)
                    for j in range(4):
                        o = 16 * g + 4 * j
                        last = mm(ps[32 * j:32 * j + 32, 4 + g % 2, :], proj_m[:], zt[:, :, o:o + 4],
                                  start=True, stop=True)
                    last.then_inc(raw_mm, 1)
                    if g >= 1:
                        turn(g - 1)
                turn(GROUPS - 1)

            def corr(k, front_too):
                def split_turn(q, half):
                    if half == 0:
                        pe.wait_ge(low_set, k * CHUNKS + q + 1)
                    if q >= 1:
                        pe.wait_ge(split_sb, k * 2 * CHUNKS + 2 * q - 1 + half)
                    for o in range(HC):
                        last = tr(turned_parts[half][:, o, :],
                                  parts[q % 2][:, HC * half + o, :, :].rearrange("p k r -> p (k r)"), ident_bf[:])
                    last.then_inc(split_mm, 1)

                def add_up(q, half):
                    if q >= 1:
                        pe.wait_ge(corr_add, k * 2 * CHUNKS + 2 * q - 1 + half)
                    pe.wait_ge(split_sb, k * 2 * CHUNKS + 2 * q + half + 1)
                    for o in range(HC * half, HC * (half + 1)):
                        if o % 4 == 0:
                            mm(ps[:, o // 4, :], waves_m[:], spread[:, o:o + 4, :].rearrange("p o f -> p (o f)"),
                               start=True, stop=True)
                        last = mm(ps[:, o // 4, P * (o % 4):P * (o % 4 + 1)], spread[:, o, :], waves_n[:],
                                  start=False, stop=True, skip_group_check=True)
                    last.then_inc(corr_mm, 1)

                pe.wait_ge(trn_sb, front_base(k) + 2 * GROUPS)
                pe.wait_ge(turn_read, k + 1)
                for q in range(-1, CHUNKS):
                    g = EARLY_FRONT + q + 1
                    for half in range(2):
                        if q + 1 < CHUNKS:
                            split_turn(q + 1, half)
                        if q >= 0:
                            add_up(q, half)
                        if front_too and g < GROUPS:
                            (front_project, front_turn)[half](k + 1, g)

            def turn(k, t):
                for h in range(CH):
                    if t == 0:
                        if h == 0:
                            pe.wait_ge(corr_add, (k + 1) * 2 * CHUNKS)
                    else:
                        pe.wait_ge(out_add, k * TURNS + 2 * t - 1 + h)
                    for i in range(ROWS):
                        last = tr(ps[:, 2 + h, P * i:P * (i + 1)], zt[:, ROWS * t + i, P * h:P * (h + 1)], ident[:])
                    last.then_inc(turn_mm, 1)

            def mix(k, t):
                u = TILES + t
                pe.wait_ge(xin_in[u % XS], 16 * (k * ring_tiles + u // XS + 1))
                for pair in range(2):
                    if t >= 1:
                        pe.wait_ge(z_sb, k * TURNS + 2 * t - 1 + pair)
                    for i in range(2):
                        for h in range(CH):
                            row = 512 * h + P * (2 * pair + i)
                            last = mm(ps[:, pair, C * i:C * (i + 1)], xin[:, u % XS, row:row + P],
                                      wrt_sb[:, h, :], start=(h == 0), stop=(h == CH - 1))
                    last.then_inc(z_mm, 1)

            def small(k, t):
                if t == 0:
                    pe.wait_ge(trn_sb, front_base(k) + GROUPS)
                    for h in range(CH):
                        for r in range(NR):
                            last = mm(ps[:, 5, 49 * h + NR * r:49 * h + NR * (r + 1)], beta[:, r, P * h:P * (h + 1)],
                                      proj_n[:, 0:NR], start=True, stop=True)
                    last.then_inc(stat_mm, 1)
                if t < NR:
                    if t >= 1:
                        pe.wait_ge(bturn_sb, k * NR + t)
                    for h in range(CH):
                        last = tr(ps[:, 6, P * h:P * (h + 1)], beta[:, NR + t, P * h:P * (h + 1)], ident[:])
                    last.then_inc(bturn_mm, 1)
                if 1 <= t <= NR:
                    r = t - 1
                    pe.wait_ge(bturn_sb, k * NR + t)
                    if r >= 1:
                        pe.wait_ge(bmix_sb, k * NR + r)
                    for h in range(CH):
                        last = mm(ps[:, 4, 0:C], raw[:, r % 2, P * h:P * (h + 1)], wrt_sb[:, h, :],
                                  start=(h == 0), stop=(h == CH - 1))
                    last.then_inc(bmix_mm, 1)
                if t == 3:
                    pe.wait_ge(mag_set, k + 1)
                    for h in range(CH):
                        last = mm(ps[0:CENTRE_PAIRS, 5, 100:101], mag[:, h, :], mean[:],
                                  start=(h == 0), stop=(h == CH - 1))
                    last.then_inc(cen_mm, 1)
                if t == 4:
                    pe.wait_ge(cen_set, k + 1)
                    own_wait(pe)
                    mm(ps[0:32, 5, 104:105], w1a_sb[:], cen[:], start=True, stop=False)
                    mm(ps[0:32, 5, 104:105], w1b_sb[:], cen[0:CENTRE_PAIRS - 1, :],
                       start=False, stop=True).then_inc(hid_mm, 1)
                if t == 5:
                    pe.wait_ge(hid_set, k + 1)
                    mm(ps[:, 5, 108:111], hid_rep, w2_sb[:], start=True, stop=False)
                    mm(ps[:, 5, 108:111], ones[0:1, :], b2_sb[:], start=False, stop=True).then_inc(par_mm, 1)
                if t == 9:
                    pe.wait_ge(kern_set, k + 1)
                    for s in range(2):
                        mm(ps[:, 5, 128 + 8 * s:135 + 8 * s], trig[:, s, :], kern[0:KS, 56:63], start=True, stop=True)
                        mm(ps[:, 5, 144 + 8 * s:151 + 8 * s], trig[:, s, :], kern[0:KS, 49:56], start=True, stop=True)
                        last = mm(ps[0:KS, 5, 256 + P * s:256 + P * (s + 1)], kern[0:KS, 56:63], trig[:, s, :],
                                  start=True, stop=True)
                    last.then_inc(tab_mm, 1)
                if t == 10:
                    pe.wait_ge(tab_set, k + 1)
                    for s in range(2):
                        last = mm(ps[:, 5, 0:H], ptab[:, s, :], trig[:, s, :], start=(s == 0), stop=(s == 1))
                    last.then_inc(w_mm, 1)
                if t == 11:
                    pe.wait_ge(bmix_sb, (k + 1) * NR)
                    for h in range(CH):
                        for r in range(NR):
                            last = mm(ps[:, 7, 49 * h + NR * r:49 * h + NR * (r + 1)], gd[:, NR + r, P * h:P * (h + 1)],
                                      proj_m[:, 0:NR], start=True, stop=True)
                    last.then_inc(eps_mm, 1)
                if t == 12:
                    pe.wait_ge(eps_set, k + 1)
                    own_wait(pe)
                    for h in range(CH):
                        last = tr(ps[0:49, 7, 256 + P * h - 128:256 + P * h], eps_sb[:, h, :], ident[:])
                    last.then_inc(epst_mm, 1)
                if 16 <= t < 20:
                    i = t - 16
                    rows = range(2 * i, min(2 * i + 2, NR))
                    if i == 0:
                        pe.wait_ge(epst_set, k + 1)
                        pe.wait_ge(cmap_set, k + 1)
                    else:
                        pe.wait_ge(kap_sb, 4 * k + i)
                    own_wait(pe)
                    for r in rows:
                        last = mm(ps[0:NR, 6, C * (r % 2):C * (r % 2 + 1)], cmap[:, NR * r:NR * (r + 1)], eps_t,
                                  start=True, stop=True)
                    last.then_inc(kap_mm, 1)
                    pe.wait_ge(kap_sb, 4 * k + i + 1)
                    if i >= 1:
                        pe.wait_ge(init_sb, 4 * k + i)
                    mm(ps[:, 7, 0:C * len(rows)], nyq_t[:], raw[0:NR, i % 2, 0:C * len(rows)],
                       start=True, stop=True).then_inc(init_mm, 1)

            pe.wait_ge(const_in, CONST_READY)
            pe.wait_ge(const_set, 2)
            for g in range(GROUPS):
                front_project(0, g)
                front_turn(0, g)
            for t in range(TILES):
                mix(0, t)
                small(0, t)
            with pe.Fori(0, NB - 1) as k:
                project_m(k)
                for g in range(EARLY_FRONT):
                    front_project(k + 1, g)
                    front_turn(k + 1, g)
                corr(k, True)
                for t in range(TILES):
                    turn(k, t)
                    mix(k + 1, t)
                    small(k + 1, t)
            project_m(NB - 1)
            corr(NB - 1, False)
            for t in range(TILES):
                turn(NB - 1, t)

        @block_ctx.scalar
        def _(act):
            def copy(o, i):
                return nc.scalar.activation(o, i, ACT.Copy)

            def group_to_sbuf(base, g, bank):
                act.wait_ge(raw_mm, base + g + 1)
                if g >= 2:
                    act.wait_ge(trn_mm, base + g - 1)
                copy(raw[:, g % 2, :], ps[:, bank, :]).then_inc(raw_sb, 1)

            def turned_group(base, g, bank, rows, dst):
                act.wait_ge(trn_mm, base + g + 1)
                copy(dst[:, :, 16 * g:16 * g + 16].rearrange("p r (j i) -> p r j i", j=4),
                     ps[:, bank, :].rearrange("p (i j r) -> p r j i", i=4, j=4)[:, 0:rows, :, :])\
                    .then_inc(trn_sb, 1)

            def front_group(k, g):
                group_to_sbuf(front_base(k), g, 6)

            def front_turned(k, g):
                turned_group(front_base(k), g, 7, 2 * NR, beta[:, :, :])

            def project_m(k):
                base = front_base(k) + GROUPS
                act.wait_ge(dproj_free, k + 1)
                for g in range(GROUPS):
                    group_to_sbuf(base, g, 4 + g % 2)
                    if g >= 1:
                        turned_group(base, g - 1, (g - 1) % 2, NR, dproj[:, :, :])
                turned_group(base, GROUPS - 1, (GROUPS - 1) % 2, NR, dproj[:, :, :])

            def corr(k, front_too):
                gv = gd[:, :, :].rearrange("p r o -> p o r")

                def lead(q):
                    if q >= 2:
                        act.wait_ge(split_mm, k * 2 * CHUNKS + 2 * q - 2)
                    src = gv[:, QC * q:QC * (q + 1), :].unsqueeze(2).broadcast_to([P, QC, 3, 2 * NR])
                    copy(parts[q % 2][:, :, 0:3, :], src).then_inc(lead_set, 1)

                def middle(q):
                    act.wait_ge(rest_set, k * CHUNKS + q + 1)
                    src = rest[:, q % 2, :, :].unsqueeze(2).broadcast_to([P, QC, 2, 2 * NR])
                    copy(parts[q % 2][:, :, 3:5, :], src).then_inc(mid_set, 1)

                def turned(q, half):
                    act.wait_ge(split_mm, k * 2 * CHUNKS + 2 * q + half + 1)
                    if q >= 1:
                        act.wait_ge(corr_mm, k * 2 * CHUNKS + 2 * q - 1 + half)
                    copy(spread[:, HC * half:HC * (half + 1), :], turned_parts[half]).then_inc(split_sb, 1)

                act.wait_ge(gamma_done, k + 1)
                act.wait_ge(delta_done, k + 1)
                act.wait_ge(shared_free, k + 1)
                lead(0)
                lead(1)
                middle(0)
                for q in range(-1, CHUNKS):
                    g = EARLY_FRONT + q + 1
                    if q + 1 < CHUNKS:
                        turned(q + 1, 0)
                    if front_too and EARLY_FRONT < g <= GROUPS:
                        front_turned(k + 1, g - 1)
                    if q + 2 < CHUNKS:
                        middle(q + 2)
                    if front_too and g < GROUPS:
                        front_group(k + 1, g)
                    if q + 1 < CHUNKS:
                        turned(q + 1, 1)
                    if q + 3 < CHUNKS:
                        lead(q + 3)

            def z_rows(k, t):
                for pair in range(2):
                    act.wait_ge(z_mm, k * TURNS + 2 * t + pair + 1)
                    n = ROWS * t + 2 * pair
                    copy(zt[:, n:n + 2, :], ps[:, pair, :].rearrange("p (n o) -> p n o", n=2)).then_inc(z_sb, 1)

            def small(k, t):
                if t < NR:
                    act.wait_ge(bturn_mm, k * NR + t + 1)
                    if t >= 2:
                        act.wait_ge(bmix_mm, k * NR + t - 1)
                    copy(raw[:, t % 2, 0:C], ps[:, 6, 0:C]).then_inc(bturn_sb, 1)
                if 1 <= t <= NR:
                    act.wait_ge(bmix_mm, k * NR + t)
                    copy(gd[:, NR + t - 1, :], ps[:, 4, 0:C]).then_inc(bmix_sb, 1)
                if t == 2:
                    act.wait_ge(stat_sq, k + 1)
                    nc.scalar.activation(mag, re, ACT.Sqrt).then_inc(mag_set, 1)
                if t == 5:
                    act.wait_ge(rsq_set, k + 1)
                    nc.scalar.activation(pc[:, 14:15], pc[:, 13:14], ACT.Sqrt).then_inc(rad_set, 1)
                if t == 6:
                    act.wait_ge(hsq_set, k + 1)
                    nc.scalar.activation(pc[:, 20:21], pc[:, 19:20], ACT.Sqrt).then_inc(half_set, 1)
                    nc.scalar.activation(pc[:, 27:28], pc[:, 2:3], ACT.Exp).then_inc(lam_set, 1)
                if t == 7:
                    act.wait_ge(expo_set, k + 1)
                    nc.scalar.activation(g4, g3, ACT.Exp, scale=-1.0).then_inc(exp_set, 1)
                if t == 10:
                    act.wait_ge(w_mm, k + 1)
                    copy(wt[:], ps[:, 5, 0:H]).then_inc(w_set, 1)
                if t == 12:
                    act.wait_ge(epst_mm, k + 1)
                    copy(eps_t, ps[0:49, 7, 128:384]).then_inc(epst_set, 1)
                if 16 <= t < 20:
                    i = t - 16
                    nr = len(range(2 * i, min(2 * i + 2, NR)))
                    act.wait_ge(kap_mm, 4 * k + i + 1)
                    if i >= 2:
                        act.wait_ge(init_mm, 4 * k + i - 1)
                    copy(raw[0:NR, i % 2, 0:C * nr], ps[0:NR, 6, 0:C * nr]).then_inc(kap_sb, 1)
                    act.wait_ge(init_mm, 4 * k + i + 1)
                    copy(gd[:, 2 * i:2 * i + nr, :], ps[:, 7, 0:C * nr].rearrange("p (r o) -> p r o", r=nr))\
                        .then_inc(init_sb, 1)

            for g in range(GROUPS):
                front_group(0, g)
                front_turned(0, g)
            for t in range(TILES):
                z_rows(0, t)
                small(0, t)
            with act.Fori(0, NB - 1) as k:
                project_m(k)
                for g in range(EARLY_FRONT):
                    front_group(k + 1, g)
                    front_turned(k + 1, g)
                corr(k, True)
                for t in range(TILES):
                    z_rows(k + 1, t)
                    small(k + 1, t)
            project_m(NB - 1)
            corr(NB - 1, False)

        @block_ctx.vector
        def _(dve):
            ts, tt = nc.vector.tensor_scalar, nc.vector.tensor_tensor
            stt, cp = nc.vector.scalar_tensor_tensor, nc.vector.tensor_copy
            step = [0]

            def restart():
                dve.sem_clear(dve_step)
                step[0] = 0

            def mark(ins):
                step[0] += 1
                ins.then_inc(dve_step, 1)

            def settle():
                dve.wait_ge(dve_step, step[0])

            def link(ins):
                mark(ins)
                settle()

            nc.vector.memset(ones[:], 1.0).then_inc(const_set, 1)
            nc.vector.memset(mean[:], 1.0 / (P * C)).then_inc(const_set, 1)
            dve.wait_ge(const_in, CONST_READY)
            dve.wait_ge(const_set, 2)

            def col(i, j=None):
                return pc[:, i:(i + 1 if j is None else j)]

            def spectrum(k):
                dve.wait_ge(stat_mm, k + 1)
                link(cp(spec, ps[:, 5, 0:98].rearrange("p (h f) -> p h f", h=CH)))
                v = spec.rearrange("p h (r s) -> p h r s", r=NR)
                c_, s_ = slice(1, NR, 2), slice(2, NR, 2)
                cc, ss, cs, sc = v[:, :, c_, c_], v[:, :, s_, s_], v[:, :, c_, s_], v[:, :, s_, c_]

                def grid_of(t, side):
                    a = t[:, :, 3:24].rearrange("p h (a b) -> p h a b", a=R)
                    return a[:, :, :, 4:7] if side > 0 else a[:, :, :, 2::-1]
                mark(nc.vector.memset(im[:, :, 24:25], 0.0))
                mark(cp(re[:, :, 24:25], v[:, :, 0, 0:1]))
                mark(cp(re[:, :, 0:3], v[:, :, 0, c_]))
                mark(cp(im[:, :, 0:3], v[:, :, 0, s_]))
                mark(cp(re[:, :, 6:24:7], v[:, :, c_, 0]))
                mark(cp(im[:, :, 6:24:7], v[:, :, s_, 0]))
                mark(tt(grid_of(re, 1), cc, ss, ALU.subtract))
                mark(tt(grid_of(re, -1), cc, ss, ALU.add))
                mark(tt(grid_of(im, 1), cs, sc, ALU.add))
                mark(tt(grid_of(im, -1), cs, sc, ALU.subtract))
                settle()
                mark(tt(re, re, re, ALU.mult))
                mark(tt(im[:, :, 0:24], im[:, :, 0:24], im[:, :, 0:24], ALU.mult))
                settle()
                tt(re, re, im, ALU.add).then_inc(stat_sq, 1)

            def centre(k):
                dve.wait_ge(cen_mm, k + 1)
                cp(cen[:], ps[0:CENTRE_PAIRS, 5, 100:101]).then_inc(cen_set, 1)

            def hidden(k):
                dve.wait_ge(hid_mm, k + 1)
                link(ts(hid[:], ps[0:32, 5, 104:105], b1_sb[:], 0.0, ALU.add, ALU.max))
                ts(hid_rep, ones[:], hid[:], None, ALU.mult).then_inc(hid_set, 1)

            def direction(k):
                dve.wait_ge(par_mm, k + 1)
                link(cp(col(0, 3), ps[:, 5, 108:111]))
                link(stt(col(3, 5), col(0, 2), -1.0, col(0, 2), ALU.mult, ALU.max))
                link(tt(col(5), col(3), col(4), ALU.max))
                link(ts(col(6), col(5), 0.0, None, ALU.is_equal))
                link(tt(col(7), col(5), col(6), ALU.add))
                link(nc.vector.reciprocal(col(8), col(7)))
                link(ts(col(9, 11), col(0, 2), col(8), None, ALU.mult))
                link(tt(col(10), col(10), col(6), ALU.add))
                link(tt(col(11, 13), col(9, 11), col(9, 11), ALU.mult))
                tt(col(13), col(11), col(12), ALU.add).then_inc(rsq_set, 1)

            def half_angle(k):
                dve.wait_ge(rad_set, k + 1)
                link(nc.vector.reciprocal(col(15), col(14)))
                link(ts(col(16, 18), col(9, 11), col(15), None, ALU.mult))
                link(stt(col(18), col(17), -1.0, col(17), ALU.mult, ALU.max))
                ts(col(19), col(18), 0.5, 0.5, ALU.mult, ALU.add).then_inc(hsq_set, 1)

            def exponents(k):
                dve.wait_ge(half_set, k + 1)
                dve.wait_ge(lam_set, k + 1)
                link(nc.vector.reciprocal(col(21), col(20)))
                link(stt(col(22), col(16), 0.5, col(21), ALU.mult, ALU.mult))
                mark(ts(col(23), col(17), 0.0, None, ALU.is_ge))
                mark(tt(col(24), col(20), col(22), ALU.subtract))
                mark(tt(col(28), col(27), col(27), ALU.mult))
                mark(ts(col(30), col(27), EPS, None, ALU.add))
                settle()
                mark(stt(col(25), col(24), col(23), col(22), ALU.mult, ALU.add))
                mark(stt(col(26), col(24), col(23), col(20), ALU.mult, ALU.subtract))
                mark(ts(col(28), col(28), 2.0, None, ALU.mult))
                mark(nc.vector.reciprocal(col(31), col(30)))
                settle()
                mark(nc.vector.reciprocal(col(29), col(28)))
                mark(tt(col(32), col(31), col(31), ALU.mult))
                mark(ts(g1, grid[:, 1, :], col(25), None, ALU.mult))
                mark(ts(g2, grid[:, 0, :], col(25), None, ALU.mult))
                settle()
                mark(ts(col(32), col(32), 2.0, None, ALU.mult))
                mark(stt(g3, grid[:, 0, :], col(26), g1, ALU.mult, ALU.add))
                mark(stt(g4, grid[:, 1, :], col(26), g2, ALU.mult, ALU.subtract))
                settle()
                mark(nc.vector.reciprocal(col(33), col(32)))
                mark(tt(g1, g3, g3, ALU.mult))
                mark(tt(g2, g4, g4, ALU.mult))
                settle()
                link(ts(g2, g2, col(33), None, ALU.mult))
                stt(g3, g1, col(29), g2, ALU.mult, ALU.add).then_inc(expo_set, 1)

            def normalise(k):
                dve.wait_ge(exp_set, k + 1)
                link(nc.vector.tensor_reduce(col(34), g4[:, 0:49], AX.X, ALU.add))
                link(ts(col(35), col(34), EPS, None, ALU.add))
                link(nc.vector.reciprocal(col(36), col(35)))
                ts(kern, g4, col(36), None, ALU.mult).then_inc(kern_set, 1)
                dve.wait_ge(kern_set, k + 1)

            def corner_map(k):
                for i, (a, b) in enumerate(CORNER_PAIRS):
                    kv = kern[0:49, KS * a + b:KS * a + b + 1]
                    if i == 0:
                        link(ts(cmap, corner[:, 0, :], kv, None, ALU.mult))
                    elif i < len(CORNER_PAIRS) - 1:
                        link(stt(cmap, corner[:, i, :], kv, cmap, ALU.mult, ALU.add))
                    else:
                        stt(cmap, corner[:, i, :], kv, cmap, ALU.mult, ALU.add).then_inc(cmap_set, 1)

            def scale_tables(k):
                dve.wait_ge(tab_mm, k + 1)
                for axis in range(2):
                    src = ps[:, 5, 128 + 16 * axis:144 + 16 * axis].rearrange("p (t d) -> p t d", t=2)[:, :, 4:7]
                    for i, s in enumerate(SCALES):
                        mark(ts(kn[:, axis, i, :].rearrange("p (t d) -> p t d", t=2), src, s / P, None, ALU.mult))
                mark(cp(ptab[:, 0, :], ps[0:KS, 5, 256:384]))
                mark(ts(ptab[:, 1, :], ps[0:KS, 5, 384:512], -1.0, None, ALU.mult))
                settle()
                dve.sem_inc(tab_set, 1)

            def eps_copy(k):
                dve.wait_ge(eps_mm, k + 1)
                cp(eps_sb, ps[:, 7, 0:98].rearrange("p (h f) -> p h f", h=CH)).then_inc(eps_set, 1)

            def multiply_rows(axis, src, dst_row, fresh):
                seen = set()
                for rnd in ROUNDS:
                    for row, s, part, j, p in rnd:
                        kv = kn[:, axis, SCALES.index(-s), 3 * part + j - 1:3 * part + j]
                        dst = gd[:, dst_row + row, :]
                        if fresh and row not in seen:
                            mark(ts(dst, src(p), kv, None, ALU.mult))
                        else:
                            mark(stt(dst, src(p), kv, dst, ALU.mult, ALU.add))
                        seen.add(row)
                    settle()

            def gamma(k):
                dve.wait_ge(init_sb, 4 * k + 4)
                multiply_rows(0, lambda p: gd[:, NR + p, :], 0, False)
                dve.sem_inc(gamma_done, 1)

            def delta(k):
                dve.wait_ge(trn_sb, front_base(k) + 2 * GROUPS)
                multiply_rows(1, lambda p: dproj[:, p, :], NR, True)
                dve.sem_inc(delta_done, 1)
                dve.sem_inc(dproj_free, 1)

            def weigh(k, g):
                dve.wait_ge(raw_mm, front_base(k) + GROUPS + g + 1)
                v = zt[:, :, 16 * g:16 * g + 16]
                mark(tt(v, v, wt[:].unsqueeze(2).broadcast_to([P, H, 16]), ALU.mult))

            def window(k):
                restart()
                dve.wait_ge(w_set, k + 1)
                for g in range(EARLY_ROWS):
                    weigh(k, g)
                delta(k)

            def corr(k):
                restart()

                def find_rest(q):
                    dve.wait_ge(lead_set, k * CHUNKS + q + 1)
                    if q >= 2:
                        dve.wait_ge(mid_set, k * CHUNKS + q - 1)
                        dve.wait_ge(low_set, k * CHUNKS + q - 1)
                    gv = gd[:, :, QC * q:QC * (q + 1)].rearrange("p r o -> p o r")
                    tt(rest[:, q % 2, :, :], gv, parts[q % 2][:, :, 0, :], ALU.subtract).then_inc(rest_set, 1)

                def low(q):
                    dve.wait_ge(rest_set, k * CHUNKS + q + 1)
                    dve.wait_ge(mid_set, k * CHUNKS + q + 1)
                    tt(parts[q % 2][:, :, 5, :], rest[:, q % 2, :, :], parts[q % 2][:, :, 3, :],
                       ALU.subtract).then_inc(low_set, 1)

                def add(q, half):
                    dve.wait_ge(corr_mm, (k * CHUNKS + q) * 2 + half + 1)
                    o = QC * q + HC * half
                    v = zt[:, :, o:o + HC].rearrange("p n o -> p o n")
                    tt(v, v, ps[:, 2 * half:2 * half + 2, :].rearrange("p b (o n) -> p (b o) n", n=H),
                       ALU.add).then_inc(corr_add, 1)

                find_rest(0)
                find_rest(1)
                low(0)
                for q in range(-1, CHUNKS):
                    if q >= 0:
                        if q >= EARLY_ROWS:
                            settle()
                        add(q, 0)
                    if EARLY_ROWS + q + 1 < GROUPS:
                        weigh(k, EARLY_ROWS + q + 1)
                    if q + 2 < CHUNKS:
                        low(q + 2)
                    if q >= 0:
                        add(q, 1)
                    if q + 3 < CHUNKS:
                        find_rest(q + 3)

            def out_rows(k, t):
                dve.wait_ge(xres_in[t % OS], 16 * (k * slot_tiles[t % OS] + t // OS + 1))
                for h in range(CH):
                    dve.wait_ge(turn_mm, k * TURNS + 2 * t + h + 1)
                    v = xo[:, t % OS, 512 * h:512 * (h + 1)]
                    tt(v, v, ps[:, 2 + h, :], ALU.add).then_inc(out_add, 1)

            def small(k, t):
                for at, work in ((1, spectrum), (3, centre), (4, hidden), (5, direction), (6, half_angle),
                                 (7, exponents), (8, normalise), (8, corner_map), (9, scale_tables),
                                 (11, eps_copy), (20, gamma)):
                    if t == at:
                        work(k)

            dve.sem_inc(dproj_free, 1)
            dve.sem_inc(turn_read, 1)
            restart()
            for t in range(TILES):
                small(0, t)
            with dve.Fori(0, NB - 1) as k:
                window(k)
                corr(k)
                restart()
                for t in range(TILES):
                    out_rows(k, t)
                    small(k + 1, t)
                dve.wait_ge(out_add, (k + 1) * TURNS)
                dve.sem_inc(turn_read, 1)
            window(NB - 1)
            corr(NB - 1)
            for t in range(TILES):
                out_rows(NB - 1, t)


def kernel(x, L0_conv_w1, L0_conv_b1, L0_conv_w2, L0_conv_b2, L0_conv_wr):
    import concourse.bacc as bacc
    from concourse.bass_utils import run_bass_kernel_spmd

    x = np.ascontiguousarray(x)
    w1 = np.asarray(L0_conv_w1)
    mid = 24
    arrays = {
        "x": x,
        "w1a": np.ascontiguousarray(np.concatenate([w1[mid + 1:], w1[mid:mid + 1]])),
        "w1b": np.ascontiguousarray(w1[mid - 1::-1]),
        "b1": np.ascontiguousarray(np.asarray(L0_conv_b1).reshape(32, 1)),
        "w2": np.ascontiguousarray(L0_conv_w2),
        "b2": np.ascontiguousarray(np.asarray(L0_conv_b2).reshape(1, 3)),
        "wrt": np.ascontiguousarray(np.asarray(L0_conv_wr).T.reshape(CH, P, C).transpose(1, 0, 2)),
    }
    arrays.update(tables())
    nc = bacc.Bacc("TRN2", target_bir_lowering=False, num_devices=1)
    aps = {n: nc.dram_tensor(f"in_{n}", a.shape, mybir.dt.from_np(a.dtype), kind="ExternalInput").ap()
           for n, a in arrays.items()}
    out = nc.dram_tensor("out", (NB, C, H, W), F32, kind="ExternalOutput").ap()
    own = {n: aps[n] for n in ("x", "w1a", "w1b", "b1", "w2", "b2", "wrt")}
    tab = {n: a for n, a in aps.items() if n not in own}
    build(nc, **own, tab=tab, out=out)
    r = run_bass_kernel_spmd(nc, [{f"in_{n}": a for n, a in arrays.items()}], core_ids=[0])
    return r.results[0]["out"]
```

```python
from contextlib import ExitStack

import numpy as np

import concourse.bass as bass
from concourse import mybir

F32 = mybir.dt.float32
BF16 = mybir.dt.bfloat16
ALU = mybir.AluOpType
ACT = mybir.ActivationFunctionType
AX = mybir.AxisListType

P = 128
NB, C, H, W = 8, 256, 128, 128
KS = 7
R = 3
EPS = 1e-8
TH = 2.0 * np.pi / 128
CH = C // P
NR = 7
FG = C // 32
MG = C // 64
TILES = 32
ROWS = H // TILES
XS = 4
OS = 3
QC = 16
HC = QC // 2
CHUNKS = C // QC
DEL_GROUPS = [(0, 1), (1, 2), (2, 4)]
REPS = 6
KROWS = REPS * 2 * NR
PARTS = [(0, 0), (0, 1), (0, 2), (1, 0), (1, 1), (2, 0)]
CENTRE_PAIRS = 25
TERMS = [(0, 1, 0, 1, 1), (0, -1, 1, 1, 2), (0, 1, 0, 2, 3), (0, -1, 1, 2, 4), (0, 1, 0, 3, 5), (0, -1, 1, 3, 6),
         (1, 1, 0, 1, 0), (1, 2, 0, 2, 1), (1, -2, 1, 2, 2), (1, 2, 0, 3, 3), (1, -2, 1, 3, 4),
         (2, -1, 1, 1, 0), (2, -2, 0, 2, 2), (2, -2, 1, 2, 1), (2, -2, 0, 3, 4), (2, -2, 1, 3, 3),
         (3, 1, 0, 2, 0), (3, 2, 0, 3, 1), (3, -2, 1, 3, 2),
         (4, -1, 1, 2, 0), (4, -2, 0, 3, 2), (4, -2, 1, 3, 1),
         (5, 1, 0, 3, 0), (6, -1, 1, 3, 0)]
SCALES = [-1, 1, -2, 2]


def term_rounds():
    rounds, left = [], list(TERMS)
    while left:
        seen, now = set(), []
        for t in list(left):
            if t[0] not in seen:
                seen.add(t[0])
                now.append(t)
                left.remove(t)
        rounds.append(now)
    return rounds


ROUNDS = term_rounds()


def waves(sign):
    n = np.arange(P)
    s = np.where(n % 2 == 1, float(sign), 1.0)
    cols = [s]
    for q in range(1, R + 1):
        cols += [s * np.cos(TH * q * n), s * np.sin(TH * q * n)]
    return np.stack(cols, 1)


def wrapped():
    v = np.zeros((KS, NR, NR), complex)

    def wave(q, s):
        u = np.zeros(NR, complex)
        if q == 0:
            u[0] = 1
        else:
            u[2 * abs(q) - 1] = 1
            u[2 * abs(q)] = s * 1j * np.sign(q)
        return u

    for j in range(-R, R + 1):
        for q in range(-R, R + 1):
            src = q + j
            if -R <= src <= R and ((j > 0 and q < 0 <= src) or (j < 0 and q >= 0 > src)):
                v[j + R] += np.outer(wave(q, 1), wave(src, -1)) / P
    return v


CORNER_PAIRS = [(a, b) for a in range(R + 1, KS) for b in range(KS) if b != R]


def bf16_bits(a):
    bits = a.astype(np.float32).view(np.uint32).astype(np.uint64)
    return ((bits + 0x7FFF + ((bits >> 16) & 1)) >> 16).astype(np.uint16)


def bf16_parts(a):
    parts, rest = [], a.astype(np.float64)
    for _ in range(3):
        p = (bf16_bits(rest).astype(np.uint32) << 16).view(np.float32).astype(np.float64)
        parts.append(p)
        rest = rest - p
    return parts


def tables():
    low, nyq = waves(1), waves(-1)
    m, d = np.arange(P), np.arange(-R, R + 1)
    proj_n = np.zeros((2, P // 2, 2, 32))
    both = np.concatenate([low, nyq], 1).reshape(P // 2, 2, 2 * NR)
    for a in range(2):
        proj_n[a, :, :, 16 * a:16 * a + 2 * NR] = both
    proj_m = np.zeros((P, 4, 32))
    for s in range(4):
        proj_m[:, s, 8 * s:8 * s + NR] = nyq
    trig = np.stack([np.cos(TH * np.outer(d, m)), np.sin(TH * np.outer(d, m))], 1)
    xx, yy = np.zeros((P, 63)), np.zeros((P, 63))
    f = np.arange(49)
    xx[:, :49], yy[:, :49] = f % KS - R, f // KS - R
    xx[:KS, 49:56], yy[:KS, 49:56] = d[None, :], d[:, None]
    xx[:KS, 56:63], yy[:KS, 56:63] = d[:, None], d[None, :]
    v = wrapped()
    corner = np.zeros((49, len(CORNER_PAIRS), 49))
    for i, (a, b) in enumerate(CORNER_PAIRS):
        for aa, bb in ((a, b), (KS - 1 - a, KS - 1 - b)):
            t = np.einsum("rp,sq->pqrs", v[aa], v[bb]).real
            corner[:, i, :] += t.reshape(49, 49)
    e = [p.T for p in bf16_parts(nyq)]
    waves_n = np.zeros((REPS, 2, NR, P))
    waves_m = np.zeros((REPS, 2, NR, P))
    for i, (_, part) in enumerate(PARTS):
        waves_n[i, 0] = e[part]
        waves_m[i, 1] = e[part]
    waves_n, waves_m = waves_n.reshape(KROWS, P), waves_m.reshape(KROWS, P)
    f32 = lambda a: np.ascontiguousarray(a.astype(np.float32))
    bf = lambda a: np.ascontiguousarray(bf16_bits(a))
    return {
        "proj_n": f32(proj_n.reshape(P, 2, 32)), "proj_m": f32(proj_m), "low": f32(low), "nyq": f32(nyq), "nyq_t": f32(nyq.T), "trig": f32(trig),
        "grid": f32(np.stack([xx, yy], 1)), "corner": f32(corner), "ident": f32(np.eye(P)),
        "ident_bf": bf(np.eye(P)), "waves_n": bf(waves_n), "waves_m": bf(waves_m),
    }


def build(nc, x, w1a, w1b, b1, w2, b2, wrt, tab, out):
    with ExitStack() as ctx:
        def sb(name, shape, dt=F32):
            return ctx.enter_context(nc.sbuf_tensor(name, shape, dt))

        def sem(name):
            return ctx.enter_context(nc.semaphore(name))

        zt = sb("zt", [P, H, C])
        xin = sb("xin", [P, XS, 1024])
        shared = sb("shared", [P, OS * 1024])
        xo = shared[:, :].rearrange("p (s f) -> p s f", s=OS)
        parts = [shared[:, i * 672:(i + 1) * 672].bitcast(BF16).rearrange("p (o k r) -> p o k r", o=QC, k=REPS)
                 for i in range(2)]
        spread = shared[0:KROWS, 1344:2368].bitcast(BF16).rearrange("p (o f) -> p o f", o=QC)
        rest = shared[:, 2368:2816].rearrange("p (s o r) -> p s o r", s=2, o=QC)
        beta = sb("beta", [P, 2 * NR, C])
        last_xo = beta[:, :, :].rearrange("p r o -> p (r o)")[:, 0:OS * 1024]\
            .rearrange("p (s f) -> p s f", s=OS)
        gd = sb("gd", [P, 2 * NR, C])
        dproj = sb("dproj", [P, NR, C])
        raw = sb("raw", [P, 2, 512])
        proj_n = sb("proj_n_sb", [P, 2, 32])
        proj_m = sb("proj_m_sb", [P, 4, 32])
        low = sb("low_sb", [P, NR])
        nyq = sb("nyq_sb", [P, NR])
        nyq_t = sb("nyq_t_sb", [NR, P])
        trig = sb("trig_sb", [KS, 2, P])
        grid = sb("grid_sb", [P, 2, 63])
        corner = sb("corner_sb", [49, len(CORNER_PAIRS), 49])
        ident = sb("ident_sb", [P, P])
        ident_bf = sb("ident_bf_sb", [P, P], BF16)
        waves_n = sb("waves_n_sb", [KROWS, P], BF16)
        waves_m = sb("waves_m_sb", [KROWS, P], BF16)
        wrt_sb = sb("wrt_sb", [P, CH, C])
        w1a_sb = sb("w1a_sb", [CENTRE_PAIRS, 32])
        w1b_sb = sb("w1b_sb", [CENTRE_PAIRS - 1, 32])
        b1_sb = sb("b1_sb", [32, 1])
        w2_sb = sb("w2_sb", [32, 3])
        b2_sb = sb("b2_sb", [1, 3])
        ones = sb("ones", [32, P])
        mean = sb("mean", [P, 1])
        pc = sb("pc", [P, 40])
        kn = sb("kn", [P, 2, len(SCALES), 6])
        wt = sb("wt", [P, H])
        cen = sb("cen", [CENTRE_PAIRS, 1])
        hid = sb("hid", [32, 1])
        flat = dproj[:, :, :].rearrange("p r o -> p (r o)")
        taken = [0]

        def scratch(rows, n):
            taken[0] += n
            assert taken[0] <= NR * C
            return flat[0:rows, taken[0] - n:taken[0]]

        spec = scratch(P, CH * 49).rearrange("p (h f) -> p h f", h=CH)
        re = scratch(P, CH * CENTRE_PAIRS).rearrange("p (h f) -> p h f", h=CH)
        im = scratch(P, CH * CENTRE_PAIRS).rearrange("p (h f) -> p h f", h=CH)
        mag = scratch(P, CH * CENTRE_PAIRS).rearrange("p (h f) -> p h f", h=CH)
        hid_rep = scratch(32, P)
        g1, g2, g3, g4 = (scratch(P, 63) for _ in range(4))
        kern = scratch(P, 63)
        ptab = scratch(KS, 2 * P).rearrange("p (t m) -> p t m", t=2)
        cmap = scratch(49, 49)
        eps_sb = scratch(P, CH * 49).rearrange("p (h f) -> p h f", h=CH)
        eps_t = scratch(49, C)

        ps = ctx.enter_context(nc.psum_tensor("ps", [P, 8, 512], F32))
        turned_parts = [ps[0:KROWS, 4 + i, :].bitcast(BF16).rearrange("p (o f) -> p o f", o=QC // 2) for i in range(2)]

        const_in = sem("const_in")
        first_in = sem("first_in")
        const_set = sem("const_set")
        xn_in = [sem(f"xn_in{i}") for i in range(XS)]
        xc_in = [sem(f"xc_in{i}") for i in range(XS)]
        xres_in = [sem(f"xres_in{i}") for i in range(OS)]
        stored = [sem(f"stored{i}") for i in range(OS)]
        xn_used = sem("xn_used")
        raw_mm = sem("raw_mm")
        raw_sb, trn_mm, trn_sb = sem("raw_sb"), sem("trn_mm"), sem("trn_sb")
        z_mm, z_sb = sem("z_mm"), sem("z_sb")
        turn_mm, out_add = sem("turn_mm"), sem("out_add")
        delta_done = sem("delta_done")
        weighed = sem("weighed")
        gamma_done = sem("gamma_done")
        lead_set, rest_set, mid_set, low_set = sem("lead_set"), sem("rest_set"), sem("mid_set"), sem("low_set")
        split_mm, split_sb = sem("split_mm"), sem("split_sb")
        corr_mm, corr_add = sem("corr_mm"), sem("corr_add")
        bturn_mm, bturn_sb, bmix_mm, bmix_sb = sem("bturn_mm"), sem("bturn_sb"), sem("bmix_mm"), sem("bmix_sb")
        stat_mm, stat_sq, mag_set = sem("stat_mm"), sem("stat_sq"), sem("mag_set")
        cen_mm, cen_set, hid_mm, hid_set, par_mm = sem("cen_mm"), sem("cen_set"), sem("hid_mm"), sem("hid_set"), sem("par_mm")
        rsq_set, rad_set, hsq_set, half_set, lam_set = (sem("rsq_set"), sem("rad_set"), sem("hsq_set"),
                                                        sem("half_set"), sem("lam_set"))
        expo_set, exp_set, kern_set = sem("expo_set"), sem("exp_set"), sem("kern_set")
        tab_mm, tab_set, w_mm, w_set = sem("tab_mm"), sem("tab_set"), sem("w_mm"), sem("w_set")
        eps_mm, eps_set, epst_mm, epst_set, cmap_set = (sem("eps_mm"), sem("eps_set"), sem("epst_mm"),
                                                        sem("epst_set"), sem("cmap_set"))
        kap_mm, kap_sb, init_mm, init_sb = sem("kap_mm"), sem("kap_sb"), sem("init_mm"), sem("init_sb")
        dve_step = sem("dve_step")

        shared_free = sem("shared_free")
        turn_read = sem("turn_read")
        dproj_free = sem("dproj_free")
        passed = sem("passed")

        first_consts = [(proj_n, tab["proj_n"]), (ident, tab["ident"])]
        consts = [(proj_m, tab["proj_m"]), (low, tab["low"]), (nyq, tab["nyq"]),
                  (nyq_t, tab["nyq_t"]), (trig, tab["trig"]),
                  (grid, tab["grid"]), (corner, tab["corner"]),
                  (ident_bf, tab["ident_bf"].bitcast(BF16)), (waves_n, tab["waves_n"].bitcast(BF16)),
                  (waves_m, tab["waves_m"].bitcast(BF16)), (wrt_sb, wrt),
                  (w1a_sb, w1a), (w1b_sb, w1b), (b1_sb, b1), (w2_sb, w2), (b2_sb, b2)]
        CONST_READY = 16 * len(consts)

        TURNS = 2 * TILES
        slot_tiles = [len(range(s, TILES, OS)) for s in range(OS)]
        ring_tiles = TILES // XS

        def front_base(k):
            return k * (FG + MG)

        block_ctx = ctx.enter_context(nc.Block())

        def own_wait(engine):
            engine.sem_inc(passed, 1)

        def last_tile(tensor, e):
            h, n = divmod(2 * ROWS * e, H)
            return tensor[NB - 1, P * h:P * (h + 1), n:n + 2 * ROWS, :].rearrange("c n m -> c (n m)")

        def last_tiles(q):
            return range(2 * (q - CHUNKS // 2), 2 * (q - CHUNKS // 2) + 2) if q >= CHUNKS // 2 else range(0)

        @block_ctx.sync
        def _(sp):
            for dst, src in first_consts:
                sp.dma_start(dst[:], src).then_inc(first_in, 16)

            def residual_load():
                for t in range(TILES):
                    if t >= XS:
                        sp.wait_ge(out_add, (NB - 1) * TURNS + 2 * (t - XS) + 2)
                    else:
                        sp.wait_ge(z_mm, NB * TURNS - 2 * (XS - t) + 2)
                    sp.dma_start(xin[:, t % XS, :], last_tile(x, t)).then_inc(xc_in[t % XS], 16)

            def front_load(k, first):
                for u in range(TILES):
                    if first and u == XS:
                        for dst, src in consts:
                            sp.dma_start(dst[:], src).then_inc(const_in, 16)
                    if u >= XS:
                        sp.wait_ge(xn_used, k * TILES + u - XS + 1)
                    elif not first:
                        sp.wait_ge(z_mm, k * TURNS - 2 * (XS - u) + 2)
                    channels = x[k, 16 * (u // 2):16 * (u // 2 + 1), :, :]
                    for a in range(2):
                        sp.dma_start(xin[64 * a:64 * (a + 1), u % XS, :].rearrange("p (q f) -> p q f", q=4),
                                     channels.rearrange("(q s) (p r) m -> p q s (r m)", s=4, r=2)
                                     [:, :, 2 * (u % 2) + a, :]).then_inc(xn_in[u % XS], 16)

            def mix_tile(k, t):
                sp.dma_start(xin[:, t % XS, :].rearrange("p (h f) -> p h f", h=CH),
                             x[k, :, ROWS * t:ROWS * (t + 1), :].rearrange("(h c) n m -> c h (n m)", h=CH))\
                  .then_inc(xc_in[t % XS], 16)

            def mix_load(k):
                for t in range(TILES):
                    if t >= XS:
                        sp.wait_ge(z_mm, k * TURNS + 2 * (t - XS) + 2)
                    else:
                        sp.wait_ge(xn_used, k * TILES + TILES + t - XS + 1)
                    mix_tile(k, t)

            front_load(0, True)
            mix_load(0)
            with sp.Fori(0, NB - 1) as k:
                front_load(k + 1, False)
                mix_load(k + 1)
            residual_load()

        @block_ctx.gpsimd
        def _(pool):
            def store(k, t):
                pool.wait_ge(out_add, k * TURNS + 2 * t + 2)
                own_wait(pool)
                pool.dma_start(out[k, :, ROWS * t:ROWS * (t + 1), :].rearrange("(h c) n m -> c h (n m)", h=CH),
                               xo[:, t % OS, :].rearrange("p (h f) -> p h f", h=CH)).then_inc(stored[t % OS], 16)

            def turn_io(k):
                pool.wait_ge(corr_mm, (k + 1) * 2 * CHUNKS)
                for t in range(TILES):
                    if t >= OS:
                        pool.wait_ge(stored[t % OS], 16 * (k * slot_tiles[t % OS] + t // OS))
                    own_wait(pool)
                    pool.dma_start(xo[:, t % OS, :].rearrange("p (h f) -> p h f", h=CH),
                                   x[k, :, ROWS * t:ROWS * (t + 1), :].rearrange("(h c) n m -> c h (n m)", h=CH))\
                        .then_inc(xres_in[t % OS], 16)
                    if t >= 1:
                        store(k, t - 1)
                store(k, TILES - 1)
                for s in range(OS):
                    pool.wait_ge(stored[s], 16 * (k + 1) * slot_tiles[s])
                pool.sem_inc(shared_free, 1)

            def weigh(k):
                pool.wait_ge(w_set, k + 1)
                for q in range(CHUNKS):
                    pool.wait_ge(raw_mm, k * MG + q // (64 // QC) + 1)
                    own_wait(pool)
                    v = zt[:, :, QC * q:QC * (q + 1)]
                    nc.gpsimd.tensor_tensor(v, v, wt[:].unsqueeze(2).broadcast_to([P, H, QC]), ALU.mult)\
                        .then_inc(weighed, 1)

            pool.sem_inc(shared_free, 1)
            with pool.Fori(0, NB - 1) as k:
                weigh(k)
                turn_io(k)
            weigh(NB - 1)
            for t in range(TILES):
                pool.wait_ge(out_add, (NB - 1) * TURNS + 2 * t + 2)
                pool.dma_start(last_tile(out, t), last_xo[:, t % OS, :]).then_inc(stored[t % OS], 16)
            for s in range(OS):
                pool.wait_ge(stored[s], 16 * NB * slot_tiles[s])

        @block_ctx.tensor
        def _(pe):
            mm = nc.tensor.matmul
            tr = nc.tensor.transpose

            def front_project(k, g, v, banks=(6,)):
                if g >= len(banks) and v == 0:
                    pe.wait_ge(raw_sb, front_base(k) + g + 1 - len(banks))
                bank = banks[g % len(banks)]
                for b in range(2):
                    u = 4 * g + 2 * v + b
                    pe.wait_ge(xn_in[u % XS], 32 * (k * ring_tiles + u // XS + 1))
                for r in range(2):
                    for e in range(2):
                        for b in range(2):
                            rows = xin[:, (2 * v + b) % XS, :].rearrange("p (q r m) -> p r q m", q=4, r=2)
                            j = 2 * e + b
                            last = mm(ps[32 * j:32 * j + 32, bank, 256 * v:256 * (v + 1)], proj_n[:, r, :],
                                      rows[:, r, e::2, :], start=(r == 0), stop=(r == 1))
                            if r == 1 and e == 1:
                                last.then_inc(xn_used, 1)

            def front_turn(k, g):
                pe.wait_ge(raw_sb, front_base(k) + g + 1)
                if g >= 1:
                    pe.wait_ge(trn_sb, front_base(k) + g)
                for i in range(4):
                    last = tr(ps[:, 7, P * i:P * (i + 1)], raw[:, g % 2, P * i:P * (i + 1)], ident[:])
                last.then_inc(trn_mm, 1)

            def split_turn(k, q, half):
                if half == 0:
                    pe.wait_ge(low_set, k * CHUNKS + q + 1)
                if q >= 1:
                    pe.wait_ge(split_sb, k * 2 * CHUNKS + 2 * q - 1 + half)
                for o in range(HC):
                    last = tr(turned_parts[half][:, o, :],
                              parts[q % 2][:, HC * half + o, :, :].rearrange("p k r -> p (k r)"), ident_bf[:])
                last.then_inc(split_mm, 1)

            def project_m(k):
                base = front_base(k) + FG

                def turn(g):
                    pe.wait_ge(raw_sb, base + g + 1)
                    if g >= 2:
                        pe.wait_ge(trn_sb, base + g - 1)
                    for i in range(4):
                        last = tr(ps[:, g % 2, P * i:P * (i + 1)], raw[:, g % 2, i:512:4], ident[:])
                    last.then_inc(trn_mm, 1)

                pe.wait_ge(z_sb, (k + 1) * TURNS)
                pe.wait_ge(init_sb, (k + 1) * 4)
                for g in range(MG):
                    if g >= 2:
                        pe.wait_ge(raw_sb, base + g - 1)
                    for s in range(4):
                        for j in range(4):
                            o = 64 * g + 16 * j + 4 * s
                            last = mm(ps[32 * j:32 * j + 32, 4 + g % 2, :], proj_m[:, s, :], zt[:, :, o:o + 4],
                                      start=(s == 0), stop=(s == 3))
                        if s == 3:
                            last.then_inc(raw_mm, 1)
                        if s == 0 and g >= 1:
                            turn(g - 1)
                split_turn(k, 0, 0)
                turn(MG - 1)

            def last_turn(t):
                h, n = divmod(2 * ROWS * t, H)
                if n == 0:
                    pe.wait_ge(corr_add, ((NB - 1) * CHUNKS + CHUNKS // 2 * (h + 1)) * 2)
                for i in range(2):
                    if t >= 1:
                        pe.wait_ge(out_add, (NB - 1) * TURNS + 2 * t - 1 + i)
                    for j in range(ROWS):
                        last = tr(ps[:, 6 + i, P * j:P * (j + 1)], zt[:, n + ROWS * i + j, P * h:P * (h + 1)], ident[:])
                    last.then_inc(turn_mm, 1)

            def corr(k, front_too):
                def add_up(q, half):
                    if q == 0 and half == 0:
                        pe.wait_ge(trn_sb, front_base(k) + FG + MG)
                        pe.wait_ge(turn_read, k + 1)
                    if q >= 1:
                        pe.wait_ge(corr_add, k * 2 * CHUNKS + 2 * q - 1 + half)
                    pe.wait_ge(split_sb, k * 2 * CHUNKS + 2 * q + half + 1)
                    for o in range(HC * half, HC * (half + 1)):
                        if o % 4 == 0:
                            mm(ps[:, o // 4, :], waves_m[:], spread[:, o:o + 4, :].rearrange("p o f -> p (o f)"),
                               start=True, stop=True)
                        last = mm(ps[:, o // 4, P * (o % 4):P * (o % 4 + 1)], spread[:, o, :], waves_n[:],
                                  start=False, stop=True, skip_group_check=True)
                    last.then_inc(corr_mm, 1)

                for q in range(-1, CHUNKS):
                    g, late = (q + 2) // 2, q % 2
                    for half in range(2):
                        if q + 1 < CHUNKS and (q, half) != (-1, 0):
                            split_turn(k, q + 1, half)
                        if q >= 0:
                            add_up(q, half)
                        if front_too and g <= FG and (late, half) == (0, 0):
                            front_turn(k + 1, g - 1)
                        if front_too and g < FG and (late, half) == (0, 1):
                            front_project(k + 1, g, 0)
                        if front_too and 1 <= g < FG and (late, half) == (1, 0):
                            front_project(k + 1, g, 1)
                        if front_too and q == -1:
                            front_project(k + 1, 0, half)
                        if not front_too and last_tiles(q):
                            last_turn(last_tiles(q)[half])

            def turn(k, t):
                for h in range(CH):
                    if t == 0:
                        if h == 0:
                            pe.wait_ge(corr_add, (k + 1) * 2 * CHUNKS)
                    else:
                        pe.wait_ge(out_add, k * TURNS + 2 * t - 1 + h)
                    for i in range(ROWS):
                        last = tr(ps[:, 2 + h, P * i:P * (i + 1)], zt[:, ROWS * t + i, P * h:P * (h + 1)], ident[:])
                    last.then_inc(turn_mm, 1)

            def mix(k, t):
                pe.wait_ge(xc_in[t % XS], 16 * (k * ring_tiles + t // XS + 1))
                for pair in range(2):
                    if t >= 1:
                        pe.wait_ge(z_sb, k * TURNS + 2 * t - 1 + pair)
                    for i in range(2):
                        for h in range(CH):
                            row = 512 * h + P * (2 * pair + i)
                            last = mm(ps[:, pair, C * i:C * (i + 1)], xin[:, t % XS, row:row + P],
                                      wrt_sb[:, h, :], start=(h == 0), stop=(h == CH - 1))
                    last.then_inc(z_mm, 1)

            def small(k, t):
                if t == 0:
                    pe.wait_ge(trn_sb, front_base(k) + FG)
                    for h in range(CH):
                        for r in range(NR):
                            last = mm(ps[:, 5, 49 * h + NR * r:49 * h + NR * (r + 1)], beta[:, r, P * h:P * (h + 1)],
                                      low[:], start=True, stop=True)
                    last.then_inc(stat_mm, 1)
                if t < NR:
                    if t >= 1:
                        pe.wait_ge(bturn_sb, k * NR + t)
                    for h in range(CH):
                        last = tr(ps[:, 6, P * h:P * (h + 1)], beta[:, NR + t, P * h:P * (h + 1)], ident[:])
                    last.then_inc(bturn_mm, 1)
                if 1 <= t <= NR:
                    r = t - 1
                    pe.wait_ge(bturn_sb, k * NR + t)
                    if r >= 1:
                        pe.wait_ge(bmix_sb, k * NR + r)
                    for h in range(CH):
                        last = mm(ps[:, 4, 0:C], raw[:, r % 2, P * h:P * (h + 1)], wrt_sb[:, h, :],
                                  start=(h == 0), stop=(h == CH - 1))
                    last.then_inc(bmix_mm, 1)
                if t == 3:
                    pe.wait_ge(mag_set, k + 1)
                    for h in range(CH):
                        last = mm(ps[0:CENTRE_PAIRS, 5, 100:101], mag[:, h, :], mean[:],
                                  start=(h == 0), stop=(h == CH - 1))
                    last.then_inc(cen_mm, 1)
                if t == 4:
                    pe.wait_ge(cen_set, k + 1)
                    own_wait(pe)
                    mm(ps[0:32, 5, 104:105], w1a_sb[:], cen[:], start=True, stop=False)
                    mm(ps[0:32, 5, 104:105], w1b_sb[:], cen[0:CENTRE_PAIRS - 1, :],
                       start=False, stop=True).then_inc(hid_mm, 1)
                if t == 5:
                    pe.wait_ge(hid_set, k + 1)
                    mm(ps[:, 5, 108:111], hid_rep, w2_sb[:], start=True, stop=False)
                    mm(ps[:, 5, 108:111], ones[0:1, :], b2_sb[:], start=False, stop=True).then_inc(par_mm, 1)
                if t == 9:
                    pe.wait_ge(kern_set, k + 1)
                    for s in range(2):
                        mm(ps[:, 5, 128 + 8 * s:135 + 8 * s], trig[:, s, :], kern[0:KS, 56:63], start=True, stop=True)
                        mm(ps[:, 5, 144 + 8 * s:151 + 8 * s], trig[:, s, :], kern[0:KS, 49:56], start=True, stop=True)
                        last = mm(ps[0:KS, 5, 256 + P * s:256 + P * (s + 1)], kern[0:KS, 56:63], trig[:, s, :],
                                  start=True, stop=True)
                    last.then_inc(tab_mm, 1)
                if t == 10:
                    pe.wait_ge(tab_set, k + 1)
                    for s in range(2):
                        last = mm(ps[:, 5, 0:H], ptab[:, s, :], trig[:, s, :], start=(s == 0), stop=(s == 1))
                    last.then_inc(w_mm, 1)
                if t == 11:
                    pe.wait_ge(bmix_sb, (k + 1) * NR)
                    for h in range(CH):
                        for r in range(NR):
                            last = mm(ps[:, 7, 49 * h + NR * r:49 * h + NR * (r + 1)], gd[:, NR + r, P * h:P * (h + 1)],
                                      nyq[:], start=True, stop=True)
                    last.then_inc(eps_mm, 1)
                if t == 12:
                    pe.wait_ge(eps_set, k + 1)
                    own_wait(pe)
                    for h in range(CH):
                        last = tr(ps[0:49, 7, 256 + P * h - 128:256 + P * h], eps_sb[:, h, :], ident[:])
                    last.then_inc(epst_mm, 1)
                if 17 <= t < 21:
                    i = t - 17
                    nr = min(2, NR - 2 * i)
                    pe.wait_ge(kap_sb, 4 * k + i + 1)
                    if i >= 1:
                        pe.wait_ge(init_sb, 4 * k + i)
                    mm(ps[:, 7, 0:C * nr], nyq_t[:], raw[0:NR, i % 2, 0:C * nr],
                       start=True, stop=True).then_inc(init_mm, 1)
                if 16 <= t < 20:
                    i = t - 16
                    rows = range(2 * i, min(2 * i + 2, NR))
                    if i == 0:
                        pe.wait_ge(epst_set, k + 1)
                        pe.wait_ge(cmap_set, k + 1)
                    else:
                        pe.wait_ge(kap_sb, 4 * k + i)
                    own_wait(pe)
                    for r in rows:
                        last = mm(ps[0:NR, 6, C * (r % 2):C * (r % 2 + 1)], cmap[:, NR * r:NR * (r + 1)], eps_t,
                                  start=True, stop=True)
                    last.then_inc(kap_mm, 1)

            pe.wait_ge(first_in, 16 * len(first_consts))
            for g in range(FG):
                front_project(0, g, 0, (4, 5))
                front_project(0, g, 1, (4, 5))
                if g >= 1:
                    front_turn(0, g - 1)
            front_turn(0, FG - 1)
            pe.wait_ge(const_in, CONST_READY)
            pe.wait_ge(const_set, 2)
            for t in range(TILES):
                mix(0, t)
                small(0, t)
            with pe.Fori(0, NB - 1) as k:
                project_m(k)
                corr(k, True)
                small(k + 1, 0)
                for t in range(TILES):
                    turn(k, t)
                    mix(k + 1, t)
                    if t >= 1:
                        small(k + 1, t)
            project_m(NB - 1)
            corr(NB - 1, False)
            for t in range(TILES // 2, TILES):
                last_turn(t)

        @block_ctx.scalar
        def _(act):
            def copy(o, i):
                return nc.scalar.activation(o, i, ACT.Copy)

            def group_to_sbuf(base, g, bank):
                if g >= 2:
                    act.wait_ge(trn_mm, base + g - 1)
                copy(raw[:, g % 2, :], ps[:, bank, :]).then_inc(raw_sb, 1)

            def turned_group(base, g, bank, sets, dst):
                act.wait_ge(trn_mm, base + g + 1)
                copy(dst, ps[:, bank, :].rearrange("p (i j r) -> p r j i", i=4, j=sets)[:, 0:dst.shape[1], :, :])\
                    .then_inc(trn_sb, 1)

            def front_group(k, g, bank=6):
                act.wait_ge(xn_used, k * TILES + 4 * (g + 1))
                group_to_sbuf(front_base(k), g, bank)

            def front_turned(k, g):
                turned_group(front_base(k), g, 7, 8,
                             beta[:, :, 32 * g:32 * (g + 1)].rearrange("p r (i j) -> p r j i", i=4))

            gv = gd[:, :, :].rearrange("p r o -> p o r")

            def lead(k, q):
                for part, (first, _) in enumerate(DEL_GROUPS):
                    if q * QC == 64 * first:
                        act.wait_ge(delta_done, len(DEL_GROUPS) * k + part + 1)
                if q >= 2:
                    act.wait_ge(split_mm, k * 2 * CHUNKS + 2 * q - 2)
                src = gv[:, QC * q:QC * (q + 1), :].unsqueeze(2).broadcast_to([P, QC, 3, 2 * NR])
                copy(parts[q % 2][:, :, 0:3, :], src).then_inc(lead_set, 1)

            def middle(k, q):
                act.wait_ge(rest_set, k * CHUNKS + q + 1)
                src = rest[:, q % 2, :, :].unsqueeze(2).broadcast_to([P, QC, 2, 2 * NR])
                copy(parts[q % 2][:, :, 3:5, :], src).then_inc(mid_set, 1)

            def project_m(k):
                base = front_base(k) + FG

                def turned(g):
                    turned_group(base, g, g % 2, 16,
                                 dproj[:, :, 64 * g:64 * (g + 1)].rearrange("p r (j i) -> p r j i", i=4))

                act.wait_ge(dproj_free, k + 1)
                for g in range(MG):
                    if g == 2:
                        act.wait_ge(gamma_done, k + 1)
                        act.wait_ge(shared_free, k + 1)
                        lead(k, 0)
                        lead(k, 1)
                        middle(k, 0)
                    act.wait_ge(raw_mm, k * MG + g + 1)
                    group_to_sbuf(base, g, 4 + g % 2)
                    turned(g)

            def corr(k, front_too):
                def turned(q, half):
                    act.wait_ge(split_mm, k * 2 * CHUNKS + 2 * q + half + 1)
                    if q >= 1:
                        act.wait_ge(corr_mm, k * 2 * CHUNKS + 2 * q - 1 + half)
                    copy(spread[:, HC * half:HC * (half + 1), :], turned_parts[half]).then_inc(split_sb, 1)

                for q in range(-1, CHUNKS):
                    g, late = (q + 2) // 2, q % 2
                    if q + 1 < CHUNKS:
                        turned(q + 1, 0)
                    if q + 2 < CHUNKS:
                        middle(k, q + 2)
                    if front_too and 1 <= g < FG and late:
                        front_group(k + 1, g)
                    if q + 1 < CHUNKS:
                        turned(q + 1, 1)
                    if front_too and g <= FG and not late:
                        front_turned(k + 1, g - 1)
                    if q + 3 < CHUNKS:
                        lead(k, q + 3)
                    if front_too and q == -1:
                        front_group(k + 1, 0)

            def z_rows(k, t):
                for pair in range(2):
                    act.wait_ge(z_mm, k * TURNS + 2 * t + pair + 1)
                    n = ROWS * t + 2 * pair
                    copy(zt[:, n:n + 2, :], ps[:, pair, :].rearrange("p (n o) -> p n o", n=2)).then_inc(z_sb, 1)

            def small(k, t):
                if t < NR:
                    act.wait_ge(bturn_mm, k * NR + t + 1)
                    if t >= 2:
                        act.wait_ge(bmix_mm, k * NR + t - 1)
                    copy(raw[:, t % 2, 0:C], ps[:, 6, 0:C]).then_inc(bturn_sb, 1)
                if 1 <= t <= NR:
                    act.wait_ge(bmix_mm, k * NR + t)
                    copy(gd[:, NR + t - 1, :], ps[:, 4, 0:C]).then_inc(bmix_sb, 1)
                if t == 2:
                    act.wait_ge(stat_sq, k + 1)
                    nc.scalar.activation(mag, re, ACT.Sqrt).then_inc(mag_set, 1)
                if t == 5:
                    act.wait_ge(rsq_set, k + 1)
                    nc.scalar.activation(pc[:, 14:15], pc[:, 13:14], ACT.Sqrt).then_inc(rad_set, 1)
                if t == 6:
                    act.wait_ge(hsq_set, k + 1)
                    nc.scalar.activation(pc[:, 20:21], pc[:, 19:20], ACT.Sqrt).then_inc(half_set, 1)
                    nc.scalar.activation(pc[:, 27:28], pc[:, 2:3], ACT.Exp).then_inc(lam_set, 1)
                if t == 7:
                    act.wait_ge(expo_set, k + 1)
                    nc.scalar.activation(g4, g3, ACT.Exp, scale=-1.0).then_inc(exp_set, 1)
                if t == 10:
                    act.wait_ge(w_mm, k + 1)
                    copy(wt[:], ps[:, 5, 0:H]).then_inc(w_set, 1)
                if t == 12:
                    act.wait_ge(epst_mm, k + 1)
                    copy(eps_t, ps[0:49, 7, 128:384]).then_inc(epst_set, 1)
                if 17 <= t < 21:
                    i = t - 17
                    nr = min(2, NR - 2 * i)
                    act.wait_ge(init_mm, 4 * k + i + 1)
                    copy(gd[:, 2 * i:2 * i + nr, :], ps[:, 7, 0:C * nr].rearrange("p (r o) -> p r o", r=nr))\
                        .then_inc(init_sb, 1)
                if 16 <= t < 20:
                    i = t - 16
                    nr = min(2, NR - 2 * i)
                    act.wait_ge(kap_mm, 4 * k + i + 1)
                    if i >= 2:
                        act.wait_ge(init_mm, 4 * k + i - 1)
                    copy(raw[0:NR, i % 2, 0:C * nr], ps[0:NR, 6, 0:C * nr]).then_inc(kap_sb, 1)

            for g in range(FG):
                front_group(0, g, 4 + g % 2)
                if g >= 1:
                    front_turned(0, g - 1)
            front_turned(0, FG - 1)
            for t in range(TILES):
                z_rows(0, t)
                small(0, t)
            with act.Fori(0, NB - 1) as k:
                project_m(k)
                corr(k, True)
                small(k + 1, 0)
                for t in range(TILES):
                    z_rows(k + 1, t)
                    if t >= 1:
                        small(k + 1, t)
            project_m(NB - 1)
            corr(NB - 1, False)

        @block_ctx.vector
        def _(dve):
            ts, tt = nc.vector.tensor_scalar, nc.vector.tensor_tensor
            stt, cp = nc.vector.scalar_tensor_tensor, nc.vector.tensor_copy
            step = [0]

            def restart():
                dve.sem_clear(dve_step)
                step[0] = 0

            def mark(ins):
                step[0] += 1
                ins.then_inc(dve_step, 1)

            def settle():
                dve.wait_ge(dve_step, step[0])

            def link(ins):
                mark(ins)
                settle()

            nc.vector.memset(ones[:], 1.0).then_inc(const_set, 1)
            nc.vector.memset(mean[:], 1.0 / (P * C)).then_inc(const_set, 1)
            dve.wait_ge(const_in, CONST_READY)
            dve.wait_ge(const_set, 2)

            def col(i, j=None):
                return pc[:, i:(i + 1 if j is None else j)]

            def spectrum(k):
                dve.wait_ge(stat_mm, k + 1)
                link(cp(spec, ps[:, 5, 0:98].rearrange("p (h f) -> p h f", h=CH)))
                v = spec.rearrange("p h (r s) -> p h r s", r=NR)
                c_, s_ = slice(1, NR, 2), slice(2, NR, 2)
                cc, ss, cs, sc = v[:, :, c_, c_], v[:, :, s_, s_], v[:, :, c_, s_], v[:, :, s_, c_]

                def grid_of(t, side):
                    a = t[:, :, 3:24].rearrange("p h (a b) -> p h a b", a=R)
                    return a[:, :, :, 4:7] if side > 0 else a[:, :, :, 2::-1]
                mark(nc.vector.memset(im[:, :, 24:25], 0.0))
                mark(cp(re[:, :, 24:25], v[:, :, 0, 0:1]))
                mark(cp(re[:, :, 0:3], v[:, :, 0, c_]))
                mark(cp(im[:, :, 0:3], v[:, :, 0, s_]))
                mark(cp(re[:, :, 6:24:7], v[:, :, c_, 0]))
                mark(cp(im[:, :, 6:24:7], v[:, :, s_, 0]))
                mark(tt(grid_of(re, 1), cc, ss, ALU.subtract))
                mark(tt(grid_of(re, -1), cc, ss, ALU.add))
                mark(tt(grid_of(im, 1), cs, sc, ALU.add))
                mark(tt(grid_of(im, -1), cs, sc, ALU.subtract))
                settle()
                mark(tt(re, re, re, ALU.mult))
                mark(tt(im[:, :, 0:24], im[:, :, 0:24], im[:, :, 0:24], ALU.mult))
                settle()
                tt(re, re, im, ALU.add).then_inc(stat_sq, 1)

            def centre(k):
                dve.wait_ge(cen_mm, k + 1)
                cp(cen[:], ps[0:CENTRE_PAIRS, 5, 100:101]).then_inc(cen_set, 1)

            def hidden(k):
                dve.wait_ge(hid_mm, k + 1)
                link(ts(hid[:], ps[0:32, 5, 104:105], b1_sb[:], 0.0, ALU.add, ALU.max))
                ts(hid_rep, ones[:], hid[:], None, ALU.mult).then_inc(hid_set, 1)

            def direction(k):
                dve.wait_ge(par_mm, k + 1)
                link(cp(col(0, 3), ps[:, 5, 108:111]))
                link(stt(col(3, 5), col(0, 2), -1.0, col(0, 2), ALU.mult, ALU.max))
                link(tt(col(5), col(3), col(4), ALU.max))
                link(ts(col(6), col(5), 0.0, None, ALU.is_equal))
                link(tt(col(7), col(5), col(6), ALU.add))
                link(nc.vector.reciprocal(col(8), col(7)))
                link(ts(col(9, 11), col(0, 2), col(8), None, ALU.mult))
                link(tt(col(10), col(10), col(6), ALU.add))
                link(tt(col(11, 13), col(9, 11), col(9, 11), ALU.mult))
                tt(col(13), col(11), col(12), ALU.add).then_inc(rsq_set, 1)

            def half_angle(k):
                dve.wait_ge(rad_set, k + 1)
                link(nc.vector.reciprocal(col(15), col(14)))
                link(ts(col(16, 18), col(9, 11), col(15), None, ALU.mult))
                link(stt(col(18), col(17), -1.0, col(17), ALU.mult, ALU.max))
                ts(col(19), col(18), 0.5, 0.5, ALU.mult, ALU.add).then_inc(hsq_set, 1)

            def exponents(k):
                dve.wait_ge(half_set, k + 1)
                dve.wait_ge(lam_set, k + 1)
                link(nc.vector.reciprocal(col(21), col(20)))
                link(stt(col(22), col(16), 0.5, col(21), ALU.mult, ALU.mult))
                mark(ts(col(23), col(17), 0.0, None, ALU.is_ge))
                mark(tt(col(24), col(20), col(22), ALU.subtract))
                mark(tt(col(28), col(27), col(27), ALU.mult))
                mark(ts(col(30), col(27), EPS, None, ALU.add))
                settle()
                mark(stt(col(25), col(24), col(23), col(22), ALU.mult, ALU.add))
                mark(stt(col(26), col(24), col(23), col(20), ALU.mult, ALU.subtract))
                mark(ts(col(28), col(28), 2.0, None, ALU.mult))
                mark(nc.vector.reciprocal(col(31), col(30)))
                settle()
                mark(nc.vector.reciprocal(col(29), col(28)))
                mark(tt(col(32), col(31), col(31), ALU.mult))
                mark(ts(g1, grid[:, 1, :], col(25), None, ALU.mult))
                mark(ts(g2, grid[:, 0, :], col(25), None, ALU.mult))
                settle()
                mark(ts(col(32), col(32), 2.0, None, ALU.mult))
                mark(stt(g3, grid[:, 0, :], col(26), g1, ALU.mult, ALU.add))
                mark(stt(g4, grid[:, 1, :], col(26), g2, ALU.mult, ALU.subtract))
                settle()
                mark(nc.vector.reciprocal(col(33), col(32)))
                mark(tt(g1, g3, g3, ALU.mult))
                mark(tt(g2, g4, g4, ALU.mult))
                settle()
                link(ts(g2, g2, col(33), None, ALU.mult))
                stt(g3, g1, col(29), g2, ALU.mult, ALU.add).then_inc(expo_set, 1)

            def normalise(k):
                dve.wait_ge(exp_set, k + 1)
                link(nc.vector.tensor_reduce(col(34), g4[:, 0:49], AX.X, ALU.add))
                link(ts(col(35), col(34), EPS, None, ALU.add))
                link(nc.vector.reciprocal(col(36), col(35)))
                ts(kern, g4, col(36), None, ALU.mult).then_inc(kern_set, 1)
                dve.wait_ge(kern_set, k + 1)

            def corner_map(k):
                for i, (a, b) in enumerate(CORNER_PAIRS):
                    kv = kern[0:49, KS * a + b:KS * a + b + 1]
                    if i == 0:
                        link(ts(cmap, corner[:, 0, :], kv, None, ALU.mult))
                    elif i < len(CORNER_PAIRS) - 1:
                        link(stt(cmap, corner[:, i, :], kv, cmap, ALU.mult, ALU.add))
                    else:
                        stt(cmap, corner[:, i, :], kv, cmap, ALU.mult, ALU.add).then_inc(cmap_set, 1)

            def scale_tables(k):
                dve.wait_ge(tab_mm, k + 1)
                for axis in range(2):
                    src = ps[:, 5, 128 + 16 * axis:144 + 16 * axis].rearrange("p (t d) -> p t d", t=2)[:, :, 4:7]
                    for i, s in enumerate(SCALES):
                        mark(ts(kn[:, axis, i, :].rearrange("p (t d) -> p t d", t=2), src, s / P, None, ALU.mult))
                mark(cp(ptab[:, 0, :], ps[0:KS, 5, 256:384]))
                mark(ts(ptab[:, 1, :], ps[0:KS, 5, 384:512], -1.0, None, ALU.mult))
                settle()
                dve.sem_inc(tab_set, 1)

            def eps_copy(k):
                dve.wait_ge(eps_mm, k + 1)
                cp(eps_sb, ps[:, 7, 0:98].rearrange("p (h f) -> p h f", h=CH)).then_inc(eps_set, 1)

            def multiply_round(i, axis, src, dst_row, fresh, cols):
                seen = {term[0] for rnd in ROUNDS[:i] for term in rnd}
                for row, s, part, j, p in ROUNDS[i]:
                    kv = kn[:, axis, SCALES.index(-s), 3 * part + j - 1:3 * part + j]
                    dst = gd[:, dst_row + row, cols]
                    if fresh and row not in seen:
                        mark(ts(dst, src[:, p, cols], kv, None, ALU.mult))
                    else:
                        mark(stt(dst, src[:, p, cols], kv, dst, ALU.mult, ALU.add))

            def gamma(k, i):
                if i == 0:
                    dve.wait_ge(init_sb, 4 * k + 4)
                settle()
                multiply_round(i, 0, gd[:, NR:2 * NR, :], 0, False, slice(0, C))
                if i == len(ROUNDS) - 1:
                    settle()
                    dve.sem_inc(gamma_done, 1)

            def delta(k, part, i):
                first, end = DEL_GROUPS[part]
                if i == 0:
                    dve.wait_ge(trn_sb, front_base(k) + FG + end)
                multiply_round(i, 1, dproj[:, :, :], NR, True, slice(64 * first, 64 * end))
                settle()
                if i == len(ROUNDS) - 1:
                    dve.sem_inc(delta_done, 1)
                    if end == MG:
                        dve.sem_inc(dproj_free, 1)

            def last_rows(t):
                k = NB - 1
                dve.wait_ge(xc_in[t % XS], 16 * (NB * ring_tiles + t // XS + 1))
                if t >= OS:
                    dve.wait_ge(stored[t % OS], 16 * (k * slot_tiles[t % OS] + t // OS))
                for h in range(CH):
                    dve.wait_ge(turn_mm, k * TURNS + 2 * t + h + 1)
                    row = slice(512 * h, 512 * (h + 1))
                    tt(last_xo[:, t % OS, row], xin[:, t % XS, row], ps[:, 6 + h, :], ALU.add).then_inc(out_add, 1)

            def corr(k, last=False):

                def find_rest(q):
                    dve.wait_ge(lead_set, k * CHUNKS + q + 1)
                    if q >= 2:
                        dve.wait_ge(mid_set, k * CHUNKS + q - 1)
                        dve.wait_ge(low_set, k * CHUNKS + q - 1)
                    gv = gd[:, :, QC * q:QC * (q + 1)].rearrange("p r o -> p o r")
                    tt(rest[:, q % 2, :, :], gv, parts[q % 2][:, :, 0, :], ALU.subtract).then_inc(rest_set, 1)

                def low(q):
                    dve.wait_ge(rest_set, k * CHUNKS + q + 1)
                    dve.wait_ge(mid_set, k * CHUNKS + q + 1)
                    tt(parts[q % 2][:, :, 5, :], rest[:, q % 2, :, :], parts[q % 2][:, :, 3, :],
                       ALU.subtract).then_inc(low_set, 1)

                def add(q, half):
                    dve.wait_ge(corr_mm, (k * CHUNKS + q) * 2 + half + 1)
                    o = QC * q + HC * half
                    v = zt[:, :, o:o + HC].rearrange("p n o -> p o n")
                    tt(v, v, ps[:, 2 * half:2 * half + 2, :].rearrange("p b (o n) -> p (b o) n", n=H),
                       ALU.add).then_inc(corr_add, 1)

                restart()
                for i in range(len(ROUNDS)):
                    delta(k, 0, i)
                find_rest(0)
                find_rest(1)
                low(0)
                for i in range(len(ROUNDS)):
                    delta(k, 1, i)
                for q in range(-1, CHUNKS):
                    if q >= 0:
                        dve.wait_ge(weighed, k * CHUNKS + q + 1)
                    if q + 2 < CHUNKS:
                        low(q + 2)
                    if q >= 0:
                        add(q, 0)
                    if q + 1 < len(ROUNDS):
                        delta(k, 2, q + 1)
                    if last and last_tiles(q):
                        last_rows(last_tiles(q)[0])
                    if q >= 0:
                        add(q, 1)
                    if q + 3 < CHUNKS:
                        find_rest(q + 3)
                    if last and last_tiles(q):
                        last_rows(last_tiles(q)[1])

            def out_rows(k, t):
                dve.wait_ge(xres_in[t % OS], 16 * (k * slot_tiles[t % OS] + t // OS + 1))
                for h in range(CH):
                    dve.wait_ge(turn_mm, k * TURNS + 2 * t + h + 1)
                    v = xo[:, t % OS, 512 * h:512 * (h + 1)]
                    tt(v, v, ps[:, 2 + h, :], ALU.add).then_inc(out_add, 1)

            def small(k, t):
                for at, work in ((1, spectrum), (3, centre), (4, hidden), (5, direction), (6, half_angle),
                                 (7, exponents), (8, normalise), (8, corner_map), (9, scale_tables),
                                 (11, eps_copy)):
                    if t == at:
                        work(k)
                if 21 <= t < 21 + len(ROUNDS):
                    gamma(k, t - 21)

            dve.sem_inc(dproj_free, 1)
            dve.sem_inc(turn_read, 1)
            restart()
            for t in range(TILES):
                small(0, t)
            with dve.Fori(0, NB - 1) as k:
                corr(k)
                restart()
                for t in range(TILES):
                    out_rows(k, t)
                    small(k + 1, t)
                dve.wait_ge(out_add, (k + 1) * TURNS)
                dve.sem_inc(turn_read, 1)
            corr(NB - 1, last=True)
            for t in range(TILES // 2, TILES):
                last_rows(t)


def kernel(x, L0_conv_w1, L0_conv_b1, L0_conv_w2, L0_conv_b2, L0_conv_wr):
    import concourse.bacc as bacc
    from concourse.bass_utils import run_bass_kernel_spmd

    x = np.ascontiguousarray(x)
    w1 = np.asarray(L0_conv_w1)
    mid = 24
    arrays = {
        "x": x,
        "w1a": np.ascontiguousarray(np.concatenate([w1[mid + 1:], w1[mid:mid + 1]])),
        "w1b": np.ascontiguousarray(w1[mid - 1::-1]),
        "b1": np.ascontiguousarray(np.asarray(L0_conv_b1).reshape(32, 1)),
        "w2": np.ascontiguousarray(L0_conv_w2),
        "b2": np.ascontiguousarray(np.asarray(L0_conv_b2).reshape(1, 3)),
        "wrt": np.ascontiguousarray(np.asarray(L0_conv_wr).T.reshape(CH, P, C).transpose(1, 0, 2)),
    }
    arrays.update(tables())
    nc = bacc.Bacc("TRN2", target_bir_lowering=False, num_devices=1)
    aps = {n: nc.dram_tensor(f"in_{n}", a.shape, mybir.dt.from_np(a.dtype), kind="ExternalInput").ap()
           for n, a in arrays.items()}
    out = nc.dram_tensor("out", (NB, C, H, W), F32, kind="ExternalOutput").ap()
    own = {n: aps[n] for n in ("x", "w1a", "w1b", "b1", "w2", "b2", "wrt")}
    tab = {n: a for n, a in aps.items() if n not in own}
    build(nc, **own, tab=tab, out=out)
    r = run_bass_kernel_spmd(nc, [{f"in_{n}": a for n, a in arrays.items()}], core_ids=[0])
    return r.results[0]["out"]
```
